# Optimizing a Trainium2 kernel written in Bass

```python
import numpy as np
import jax
import jax.numpy as jnp

def _softmax(x, axis=-1):
    return jax.nn.softmax(x, axis=axis)

def _gelu(x):
    return jax.nn.gelu(x, approximate=True)

def _silu(x):
    return jax.nn.silu(x)

def _sigmoid(x):
    return jax.nn.sigmoid(x)

def _layernorm(x, axis=-1, eps=1e-05):
    m = jnp.mean(x, axis=axis, keepdims=True)
    v = jnp.var(x, axis=axis, keepdims=True)
    return (x - m) / jnp.sqrt(v + eps)

def _scatter_add(tgt, idx, src, axis=0):
    return tgt.at[idx].add(src)

def _segment_sum(src, seg, n):
    return jax.ops.segment_sum(src, seg, n)
kernel_name = 'mk_xattn_seq_d2_seqx_r4_d4dacf'

def setup_inputs(seed: int=0):
    np.random.seed(seed)
    _w = jnp.asarray

    def _rec_inputs():
        import jax
        import jax.numpy as jnp
        _rk = jax.random.key(seed)
        x = -0.0002928 + 1 * jax.random.normal(jax.random.fold_in(_rk, 1), (2, 1024, 256), jnp.float32)
        _lenS = 1024 - jax.random.randint(jax.random.fold_in(_rk, 7), (2,), 0, max(1, 1024 // 4) + 1, jnp.int32)
        _lenS2 = 154 - jax.random.randint(jax.random.fold_in(_rk, 8), (2,), 0, max(1, 154 // 4) + 1, jnp.int32)
        _ctx_1024P = jax.random.normal(jax.random.fold_in(_rk, 11), (2, 16, 256), jnp.float32)
        _ctx_1024c = jax.random.dirichlet(jax.random.fold_in(_rk, 511), 0.3 * jnp.ones((16,), jnp.float32), (2, 154))
        _ctx_1024t = jnp.einsum('bsk,bkd->bsd', _ctx_1024c, _ctx_1024P)
        _ctx_1024t = _ctx_1024t * jax.lax.rsqrt(jnp.mean(jnp.square(_ctx_1024t)) + 1e-12) * 0.953939
        ctx_1024 = -1.39393e-06 + 0.999914 * (_ctx_1024t + 0.3 * jax.random.normal(jax.random.fold_in(_rk, 611), (2, 154, 256), jnp.float32))
        return (x, ctx_1024)
    x, ctx_1024 = _rec_inputs()

    def _L0_xattn_setup():
        import jax, jax.numpy as jnp
        import numpy as np
        B, LX, LY = (2, 512, 512)
        E, H = (256, 16)
        HD = E // H
        FF = 1024
        EPS = 1e-05

        def _rope_tables(L, d):
            inv = 1.0 / 10000.0 ** (jnp.arange(0, d, 2, dtype=jnp.float32) / d)
            t = jnp.arange(L, dtype=jnp.float32)
            f = jnp.outer(t, inv)
            return (jnp.cos(f), jnp.sin(f))

        def _apply_rope(x, cos, sin):
            d2 = x.shape[-1] // 2
            x1, x2 = (x[..., :d2], x[..., d2:])
            c = cos[None, :, None, :]
            s = sin[None, :, None, :]
            return jnp.concatenate([x1 * c - x2 * s, x2 * c + x1 * s], axis=-1)

        def _ln(x, g, b):
            m = jnp.mean(x, axis=-1, keepdims=True)
            v = jnp.var(x, axis=-1, keepdims=True)
            return (x - m) / jnp.sqrt(v + EPS) * g + b

        def _attn(q, k, v, causal):
            s = jnp.einsum('blhd,bmhd->bhlm', q, k)
            if causal:
                Lq, Lk = (s.shape[2], s.shape[3])
                mask = jnp.tril(jnp.ones((Lq, Lk), dtype=bool))
                s = jnp.where(mask, s, -jnp.inf)
            p = jax.nn.softmax(s, axis=-1)
            return jnp.einsum('bhlm,bmhd->blhd', p, v)

        def _forward(x, y, ln1_g, ln1_b, sa_wq, sa_bq, sa_wk, sa_bk, sa_wv, sa_bv, sa_wo, sa_bo, ln2_g, ln2_b, ca_wq, ca_bq, ca_wk, ca_bk, ca_wv, ca_bv, ca_wo, ca_bo, ln3_g, ln3_b, fc1_w, fc1_b, fc2_w, fc2_b):
            Bx, Lx, _ = x.shape
            Ly = y.shape[1]
            cos, sin = _rope_tables(max(Lx, Ly), HD)
            scale = HD ** (-0.5)
            h = _ln(x, ln1_g, ln1_b)
            q = (h @ sa_wq + sa_bq).reshape(Bx, Lx, H, HD) * scale
            k = (h @ sa_wk + sa_bk).reshape(Bx, Lx, H, HD)
            v = (h @ sa_wv + sa_bv).reshape(Bx, Lx, H, HD)
            q = _apply_rope(q, cos[:Lx], sin[:Lx])
            k = _apply_rope(k, cos[:Lx], sin[:Lx])
            a = _attn(q, k, v, causal=True).reshape(Bx, Lx, E)
            x = x + (a @ sa_wo + sa_bo)
            h = _ln(x, ln2_g, ln2_b)
            q = (h @ ca_wq + ca_bq).reshape(Bx, Lx, H, HD) * scale
            k = (y @ ca_wk + ca_bk).reshape(Bx, Ly, H, HD)
            v = (y @ ca_wv + ca_bv).reshape(Bx, Ly, H, HD)
            q = _apply_rope(q, cos[:Lx], sin[:Lx])
            k = _apply_rope(k, cos[:Ly], sin[:Ly])
            a = _attn(q, k, v, causal=False).reshape(Bx, Lx, E)
            x = x + (a @ ca_wo + ca_bo)
            h = _ln(x, ln3_g, ln3_b)
            return x + (jax.nn.gelu(h @ fc1_w + fc1_b) @ fc2_w + fc2_b)
        key = jax.random.key(seed)
        ks = jax.random.split(key, 16)

        def w(k, *s):
            return jax.random.normal(k, s, jnp.float32) * 0.02
        z = lambda *s: jnp.zeros(s, jnp.float32)
        o = lambda *s: jnp.ones(s, jnp.float32)
        return {'x': jax.random.normal(ks[0], (B, LX, E), jnp.float32), 'y': jax.random.normal(ks[1], (B, LY, E), jnp.float32), 'ln1_g': o(E), 'ln1_b': z(E), 'sa_wq': w(ks[2], E, E), 'sa_bq': z(E), 'sa_wk': w(ks[3], E, E), 'sa_bk': z(E), 'sa_wv': w(ks[4], E, E), 'sa_bv': z(E), 'sa_wo': w(ks[5], E, E), 'sa_bo': z(E), 'ln2_g': o(E), 'ln2_b': z(E), 'ca_wq': w(ks[6], E, E), 'ca_bq': z(E), 'ca_wk': w(ks[7], E, E), 'ca_bk': z(E), 'ca_wv': w(ks[8], E, E), 'ca_bv': z(E), 'ca_wo': w(ks[9], E, E), 'ca_bo': z(E), 'ln3_g': o(E), 'ln3_b': z(E), 'fc1_w': w(ks[10], E, FF), 'fc1_b': z(FF), 'fc2_w': w(ks[11], FF, E), 'fc2_b': z(E)}
    _L0_xattn_all = _L0_xattn_setup()
    _L0_xattn_in = {k: v for k, v in _L0_xattn_all.items() if k in ('ln1_g', 'ln1_b', 'sa_wq', 'sa_bq', 'sa_wk', 'sa_bk', 'sa_wv', 'sa_bv', 'sa_wo', 'sa_bo', 'ln2_g', 'ln2_b', 'ca_wq', 'ca_bq', 'ca_wk', 'ca_bk', 'ca_wv', 'ca_bv', 'ca_wo', 'ca_bo', 'ln3_g', 'ln3_b', 'fc1_w', 'fc1_b', 'fc2_w', 'fc2_b')}
    del _L0_xattn_all

    def _L1_xattn_setup():
        import jax, jax.numpy as jnp
        import numpy as np
        B, S, D_MODEL, H, D_FF = (2, 512, 256, 16, 1024)
        D_HEAD = D_MODEL // H
        LN_EPS = 1e-05

        def _xavier(key, shape):
            fan_out, fan_in = shape
            std = (2.0 / (fan_in + fan_out)) ** 0.5
            return jax.random.normal(key, shape, dtype=jnp.float32) * std

        def _layer_norm(x, g, b):
            mu = jnp.mean(x, axis=-1, keepdims=True)
            var = jnp.mean((x - mu) ** 2, axis=-1, keepdims=True)
            return (x - mu) * jax.lax.rsqrt(var + LN_EPS) * g + b
        key = jax.random.key(seed)
        ks = jax.random.split(key, 8)
        return {'q': jax.random.normal(ks[0], (B, S, D_MODEL), dtype=jnp.float32), 'k': jax.random.normal(ks[1], (B, S, D_MODEL), dtype=jnp.float32), 'Wq': _xavier(ks[2], (D_MODEL, D_MODEL)), 'bq': jnp.zeros((D_MODEL,), jnp.float32), 'Wk': _xavier(ks[3], (D_MODEL, D_MODEL)), 'bk': jnp.zeros((D_MODEL,), jnp.float32), 'Wv': _xavier(ks[4], (D_MODEL, D_MODEL)), 'bv': jnp.zeros((D_MODEL,), jnp.float32), 'W1': _xavier(ks[5], (D_FF, D_MODEL)), 'b1': jnp.zeros((D_FF,), jnp.float32), 'W2': _xavier(ks[6], (D_MODEL, D_FF)), 'b2': jnp.zeros((D_MODEL,), jnp.float32), 'ln_g': jnp.ones((D_MODEL,), jnp.float32), 'ln_b': jnp.zeros((D_MODEL,), jnp.float32), 'use_causal_mask': 1}
    _L1_xattn_all = _L1_xattn_setup()
    _L1_xattn_in = {k: v for k, v in _L1_xattn_all.items() if k in ('Wq', 'bq', 'Wk', 'bk', 'Wv', 'bv', 'W1', 'b1', 'W2', 'b2', 'ln_g', 'ln_b')}
    del _L1_xattn_all
    return {'x': x, 'ctx_1024': ctx_1024, 'L0_xattn_ln1_g': _L0_xattn_in['ln1_g'], 'L0_xattn_ln1_b': _L0_xattn_in['ln1_b'], 'L0_xattn_sa_wq': _L0_xattn_in['sa_wq'], 'L0_xattn_sa_bq': _L0_xattn_in['sa_bq'], 'L0_xattn_sa_wk': _L0_xattn_in['sa_wk'], 'L0_xattn_sa_bk': _L0_xattn_in['sa_bk'], 'L0_xattn_sa_wv': _L0_xattn_in['sa_wv'], 'L0_xattn_sa_bv': _L0_xattn_in['sa_bv'], 'L0_xattn_sa_wo': _L0_xattn_in['sa_wo'], 'L0_xattn_sa_bo': _L0_xattn_in['sa_bo'], 'L0_xattn_ln2_g': _L0_xattn_in['ln2_g'], 'L0_xattn_ln2_b': _L0_xattn_in['ln2_b'], 'L0_xattn_ca_wq': _L0_xattn_in['ca_wq'], 'L0_xattn_ca_bq': _L0_xattn_in['ca_bq'], 'L0_xattn_ca_wk': _L0_xattn_in['ca_wk'], 'L0_xattn_ca_bk': _L0_xattn_in['ca_bk'], 'L0_xattn_ca_wv': _L0_xattn_in['ca_wv'], 'L0_xattn_ca_bv': _L0_xattn_in['ca_bv'], 'L0_xattn_ca_wo': _L0_xattn_in['ca_wo'], 'L0_xattn_ca_bo': _L0_xattn_in['ca_bo'], 'L0_xattn_ln3_g': _L0_xattn_in['ln3_g'], 'L0_xattn_ln3_b': _L0_xattn_in['ln3_b'], 'L0_xattn_fc1_w': _L0_xattn_in['fc1_w'], 'L0_xattn_fc1_b': _L0_xattn_in['fc1_b'], 'L0_xattn_fc2_w': _L0_xattn_in['fc2_w'], 'L0_xattn_fc2_b': _L0_xattn_in['fc2_b'], 'L1_xattn_Wq': _L1_xattn_in['Wq'], 'L1_xattn_bq': _L1_xattn_in['bq'], 'L1_xattn_Wk': _L1_xattn_in['Wk'], 'L1_xattn_bk': _L1_xattn_in['bk'], 'L1_xattn_Wv': _L1_xattn_in['Wv'], 'L1_xattn_bv': _L1_xattn_in['bv'], 'L1_xattn_W1': _L1_xattn_in['W1'], 'L1_xattn_b1': _L1_xattn_in['b1'], 'L1_xattn_W2': _L1_xattn_in['W2'], 'L1_xattn_b2': _L1_xattn_in['b2'], 'L1_xattn_ln_g': _L1_xattn_in['ln_g'], 'L1_xattn_ln_b': _L1_xattn_in['ln_b']}

def reference(x, ctx_1024, L0_xattn_ln1_g, L0_xattn_ln1_b, L0_xattn_sa_wq, L0_xattn_sa_bq, L0_xattn_sa_wk, L0_xattn_sa_bk, L0_xattn_sa_wv, L0_xattn_sa_bv, L0_xattn_sa_wo, L0_xattn_sa_bo, L0_xattn_ln2_g, L0_xattn_ln2_b, L0_xattn_ca_wq, L0_xattn_ca_bq, L0_xattn_ca_wk, L0_xattn_ca_bk, L0_xattn_ca_wv, L0_xattn_ca_bv, L0_xattn_ca_wo, L0_xattn_ca_bo, L0_xattn_ln3_g, L0_xattn_ln3_b, L0_xattn_fc1_w, L0_xattn_fc1_b, L0_xattn_fc2_w, L0_xattn_fc2_b, L1_xattn_Wq, L1_xattn_bq, L1_xattn_Wk, L1_xattn_bk, L1_xattn_Wv, L1_xattn_bv, L1_xattn_W1, L1_xattn_b1, L1_xattn_W2, L1_xattn_b2, L1_xattn_ln_g, L1_xattn_ln_b):
    import jax
    import jax.numpy as jnp

    def _L0_xattn_ref(x, y, ln1_g, ln1_b, sa_wq, sa_bq, sa_wk, sa_bk, sa_wv, sa_bv, sa_wo, sa_bo, ln2_g, ln2_b, ca_wq, ca_bq, ca_wk, ca_bk, ca_wv, ca_bv, ca_wo, ca_bo, ln3_g, ln3_b, fc1_w, fc1_b, fc2_w, fc2_b):
        import jax, jax.numpy as jnp
        import numpy as np
        B, LX, LY = (2, 512, 512)
        E, H = (256, 16)
        HD = E // H
        FF = 1024
        EPS = 1e-05

        def _rope_tables(L, d):
            inv = 1.0 / 10000.0 ** (jnp.arange(0, d, 2, dtype=jnp.float32) / d)
            t = jnp.arange(L, dtype=jnp.float32)
            f = jnp.outer(t, inv)
            return (jnp.cos(f), jnp.sin(f))

        def _apply_rope(x, cos, sin):
            d2 = x.shape[-1] // 2
            x1, x2 = (x[..., :d2], x[..., d2:])
            c = cos[None, :, None, :]
            s = sin[None, :, None, :]
            return jnp.concatenate([x1 * c - x2 * s, x2 * c + x1 * s], axis=-1)

        def _ln(x, g, b):
            m = jnp.mean(x, axis=-1, keepdims=True)
            v = jnp.var(x, axis=-1, keepdims=True)
            return (x - m) / jnp.sqrt(v + EPS) * g + b

        def _attn(q, k, v, causal):
            s = jnp.einsum('blhd,bmhd->bhlm', q, k)
            if causal:
                Lq, Lk = (s.shape[2], s.shape[3])
                mask = jnp.tril(jnp.ones((Lq, Lk), dtype=bool))
                s = jnp.where(mask, s, -jnp.inf)
            p = jax.nn.softmax(s, axis=-1)
            return jnp.einsum('bhlm,bmhd->blhd', p, v)

        def _forward(x, y, ln1_g, ln1_b, sa_wq, sa_bq, sa_wk, sa_bk, sa_wv, sa_bv, sa_wo, sa_bo, ln2_g, ln2_b, ca_wq, ca_bq, ca_wk, ca_bk, ca_wv, ca_bv, ca_wo, ca_bo, ln3_g, ln3_b, fc1_w, fc1_b, fc2_w, fc2_b):
            Bx, Lx, _ = x.shape
            Ly = y.shape[1]
            cos, sin = _rope_tables(max(Lx, Ly), HD)
            scale = HD ** (-0.5)
            h = _ln(x, ln1_g, ln1_b)
            q = (h @ sa_wq + sa_bq).reshape(Bx, Lx, H, HD) * scale
            k = (h @ sa_wk + sa_bk).reshape(Bx, Lx, H, HD)
            v = (h @ sa_wv + sa_bv).reshape(Bx, Lx, H, HD)
            q = _apply_rope(q, cos[:Lx], sin[:Lx])
            k = _apply_rope(k, cos[:Lx], sin[:Lx])
            a = _attn(q, k, v, causal=True).reshape(Bx, Lx, E)
            x = x + (a @ sa_wo + sa_bo)
            h = _ln(x, ln2_g, ln2_b)
            q = (h @ ca_wq + ca_bq).reshape(Bx, Lx, H, HD) * scale
            k = (y @ ca_wk + ca_bk).reshape(Bx, Ly, H, HD)
            v = (y @ ca_wv + ca_bv).reshape(Bx, Ly, H, HD)
            q = _apply_rope(q, cos[:Lx], sin[:Lx])
            k = _apply_rope(k, cos[:Ly], sin[:Ly])
            a = _attn(q, k, v, causal=False).reshape(Bx, Lx, E)
            x = x + (a @ ca_wo + ca_bo)
            h = _ln(x, ln3_g, ln3_b)
            return x + (jax.nn.gelu(h @ fc1_w + fc1_b) @ fc2_w + fc2_b)
        return _forward(x, y, ln1_g, ln1_b, sa_wq, sa_bq, sa_wk, sa_bk, sa_wv, sa_bv, sa_wo, sa_bo, ln2_g, ln2_b, ca_wq, ca_bq, ca_wk, ca_bk, ca_wv, ca_bv, ca_wo, ca_bo, ln3_g, ln3_b, fc1_w, fc1_b, fc2_w, fc2_b)

    def _L1_xattn_ref(q, k, Wq, bq, Wk, bk, Wv, bv, W1, b1, W2, b2, ln_g, ln_b, use_causal_mask):
        import jax, jax.numpy as jnp
        import numpy as np
        B, S, D_MODEL, H, D_FF = (2, 512, 256, 16, 1024)
        D_HEAD = D_MODEL // H
        LN_EPS = 1e-05

        def _xavier(key, shape):
            fan_out, fan_in = shape
            std = (2.0 / (fan_in + fan_out)) ** 0.5
            return jax.random.normal(key, shape, dtype=jnp.float32) * std

        def _layer_norm(x, g, b):
            mu = jnp.mean(x, axis=-1, keepdims=True)
            var = jnp.mean((x - mu) ** 2, axis=-1, keepdims=True)
            return (x - mu) * jax.lax.rsqrt(var + LN_EPS) * g + b
        Bq, Sq, _ = q.shape
        Sk = k.shape[1]
        Q = q @ Wq.T + bq
        K = k @ Wk.T + bk
        V = k @ Wv.T + bv
        Q_ = Q.reshape(Bq, Sq, H, D_HEAD).transpose(0, 2, 1, 3)
        K_ = K.reshape(Bq, Sk, H, D_HEAD).transpose(0, 2, 1, 3)
        V_ = V.reshape(Bq, Sk, H, D_HEAD).transpose(0, 2, 1, 3)
        scores = jnp.einsum('bhqd,bhkd->bhqk', Q_, K_) / D_HEAD ** 0.5
        if use_causal_mask:
            causal = jnp.tril(jnp.ones((Sq, Sk), dtype=bool))
            scores = jnp.where(causal, scores, jnp.float32(-1000000000.0))
        sim = jax.nn.softmax(scores, axis=-1)
        att = jnp.einsum('bhqk,bhkd->bhqd', sim, V_)
        att_h = att.transpose(0, 2, 1, 3).reshape(Bq, Sq, D_MODEL)
        att_h = att_h + q
        att_h = _layer_norm(att_h, ln_g, ln_b)
        ff = jax.nn.gelu(att_h @ W1.T + b1, approximate=False) @ W2.T + b2
        return ff + att_h
    x = _L0_xattn_ref(x, ctx_1024, L0_xattn_ln1_g, L0_xattn_ln1_b, L0_xattn_sa_wq, L0_xattn_sa_bq, L0_xattn_sa_wk, L0_xattn_sa_bk, L0_xattn_sa_wv, L0_xattn_sa_bv, L0_xattn_sa_wo, L0_xattn_sa_bo, L0_xattn_ln2_g, L0_xattn_ln2_b, L0_xattn_ca_wq, L0_xattn_ca_bq, L0_xattn_ca_wk, L0_xattn_ca_bk, L0_xattn_ca_wv, L0_xattn_ca_bv, L0_xattn_ca_wo, L0_xattn_ca_bo, L0_xattn_ln3_g, L0_xattn_ln3_b, L0_xattn_fc1_w, L0_xattn_fc1_b, L0_xattn_fc2_w, L0_xattn_fc2_b)
    x = _L1_xattn_ref(x, ctx_1024, L1_xattn_Wq, L1_xattn_bq, L1_xattn_Wk, L1_xattn_bk, L1_xattn_Wv, L1_xattn_bv, L1_xattn_W1, L1_xattn_b1, L1_xattn_W2, L1_xattn_b2, L1_xattn_ln_g, L1_xattn_ln_b, 1)
    return x

_drawn_inputs = setup_inputs


def setup_inputs(seed=0):
    import zlib

    import numpy as np

    out = dict(_drawn_inputs(seed))
    spreads = {'L0_xattn_ln1_g': (1.0, 0.6),
     'L0_xattn_ln1_b': (0.0, 0.8),
     'L0_xattn_sa_bq': (0.0, 0.8),
     'L0_xattn_sa_bk': (0.0, 0.8),
     'L0_xattn_sa_bv': (0.0, 0.285),
     'L0_xattn_sa_bo': (0.0, 0.1),
     'L0_xattn_ln2_g': (1.0, 0.6),
     'L0_xattn_ln2_b': (0.0, 0.8),
     'L0_xattn_ca_bq': (0.0, 0.8),
     'L0_xattn_ca_bk': (0.0, 2.0),
     'L0_xattn_ca_bv': (0.0, 0.302),
     'L0_xattn_ca_bo': (0.0, 0.1),
     'L0_xattn_ln3_g': (1.0, 0.6),
     'L0_xattn_ln3_b': (0.0, 0.732),
     'L0_xattn_fc1_b': (0.0, 0.273),
     'L0_xattn_fc2_b': (0.0, 0.1),
     'L1_xattn_bq': (0.0, 0.405),
     'L1_xattn_bk': (0.0, 2.0),
     'L1_xattn_bv': (0.0, 0.1),
     'L1_xattn_b1': (0.0, 0.1),
     'L1_xattn_b2': (0.0, 0.1),
     'L1_xattn_ln_g': (1.0, 0.2),
     'L1_xattn_ln_b': (0.0, 0.1)}
    factors = {'L0_xattn_sa_wq': 8.0,
     'L0_xattn_sa_wk': 8.0,
     'L0_xattn_sa_wv': 4.721,
     'L0_xattn_ca_wq': 8.0,
     'L0_xattn_ca_wk': 8.0}
    for name, (base, spread) in spreads.items():
        noise = np.random.default_rng([zlib.crc32(name.encode()), seed]).standard_normal(out[name].shape)
        drawn = base * np.exp(spread * noise) if base else spread * noise
        out[name] = jnp.asarray(drawn.astype(out[name].dtype))
    for name, factor in factors.items():
        out[name] = (out[name] * factor).astype(out[name].dtype)
    return out
```

```python
from contextlib import ExitStack

import numpy as np
import concourse.bass as bass
from concourse import mybir

F32 = mybir.dt.float32
BF16 = mybir.dt.bfloat16
I32 = mybir.dt.int32
ALU = mybir.AluOpType
ACT = mybir.ActivationFunctionType
AX = mybir.AxisListType

P = 128
B, LX, LY, E, H, FF = 2, 1024, 154, 256, 16, 1024
HD = E // H
CH = 512
NCHUNK = B * LX // CH
NT = CH // P
HG = 4
NHG = H // HG
KT = E // P
NM = FF // P
HH = H // KT
LYB = LY - P
LYP = 160
NPROD = 6
SROW = NPROD * HD
QPART = (0, 0, 1, 0, 1, 2)
KPART = (0, 1, 0, 2, 1, 0)
NEG = -1.0e30
EPS = 1e-5
SCALE = HD ** -0.5
RSQRT_GUESS = 0x5F3759DF

BIAS_ROWS = ("sa_bv", "sa_bo", "ca_bv", "ca_bo", "fc2_b", "l1_bv", "l1_b2")
COLS = {}
for _name, _n in (("ln1_g", KT), ("ln1_b", KT), ("ln2_g", KT), ("ln2_b", KT), ("ln3_g", KT), ("ln3_b", KT),
                  ("ln4_g", KT), ("ln4_b", KT), ("sa_bq", KT), ("sa_bk", KT), ("ca_bq", KT), ("ca_bk", KT),
                  ("l1_bq", KT), ("l1_bk", KT), ("fc1_b", NM), ("l1_b1", NM)):
    COLS[_name] = (sum(n for _, n in COLS.values()), _n)
NCOLS = sum(n for _, n in COLS.values())
NROW = 4
MASKW = 2 * P + P + 2 * P


def units(att, c):
    out = []
    if att == "sa":
        half = c % 2
        for t in range(NT):
            n = (t + 1) * P
            per = {1: 4, 2: 2, 3: 1, 4: 1}[t + 1]
            for h in range(0, HG, per):
                out.append([(t, h + i, half, n, 0, i * n) for i in range(per)])
            if half:
                for h in range(HG):
                    out.append([(t, h, 0, CH, 1, 0)])
    else:
        pairs = [(t, h) for h in range(HG) for t in range(NT)]
        for i in range(0, len(pairs), 3):
            out.append([(t, h, 0, LY, 0, LYP * j) for j, (t, h) in enumerate(pairs[i:i + 3])])
    return out


def groups(att, c):
    return list(range(NT * (c % 2 + 1))) if att == "sa" else ["A", "B"]


class Order(list):

    def __init__(self):
        super().__init__()
        self.waiting = None
        self.finishing = []

    def flush_fin(self):
        for it in self.finishing:
            self.append(("turn", *it))
        self.finishing = []

    def flush_pv(self):
        if self.waiting:
            att, c, hg, g = self.waiting
            self.append(("pv", att, c, hg, g))
            self.waiting = None
            if g == groups(att, c)[-1]:
                self.append(("evac", att, c, hg))
                self.finishing.append((att, c, hg))
                return
        self.flush_fin()

    def group(self, att, c, hg, g):
        self.append(("exp", att, c, hg, g))
        self.flush_pv()
        self.waiting = (att, c, hg, g)

    def drain(self):
        self.flush_pv()
        self.flush_fin()


def maxes(att, c, hg):
    return [("max", att, c, hg, u) for u in range(len(units(att, c)))] + [("row", att, c, hg)]


def cross(att, c):
    out = []
    for f in range(KT):
        out.append(("proj", "q" + att, c, f))
        hgs = (2 * f, 2 * f + 1)
        for hg in hgs:
            out += maxes(att, c, hg)
        for hg in hgs:
            out.append(("item", att, c, hg))
    out.append(("drain",))
    return out


def post(c):
    out = [("tr", "oT_sa", c, f) for f in range(KT)]
    out += [("wo", "sa", c, g) for g in range(NT // 2)]
    out += [("stats", "ln2", c)] + [("tr", "ln2", c, f) for f in range(KT)]
    out += cross("ca", c)
    out += [("tr", "oT_ca", c, f) for f in range(KT)]
    out += [("wo", "ca", c, g) for g in range(NT // 2)]
    out += [("stats", "ln3", c)] + [("tr", "ln3", c, f) for f in range(KT)]
    out += mlp(0, c)
    out += [("tr", "x3", c, f) for f in range(KT)]
    out += cross("la", c)
    out += [("addatt", c), ("stats", "ln4", c)] + [("tr", "ln4", c, f) for f in range(KT)]
    out += [("lnout", c)]
    out += mlp(1, c)
    out += [("store", c)]
    return out


def mlp(l, c):
    out = [("up", l, c, 0)]
    for m in range(1, NM):
        out += [("up", l, c, m), ("down", l, c, m - 1)]
    out += [("down", l, c, NM - 1)]
    out += [("res", l, c, g) for g in range(NT // 2)]
    return out


def prologue(c):
    out = [("load", c), ("stats", "ln1", c)] + [("tr", "ln1", c, f) for f in range(KT)]
    out += [("proj", "ks", c, f) for f in range(KT)]
    out += [("v", c, g) for g in range(NT // 2)]
    return out


def self_q(c):
    return [("proj", "qs", c, f) for f in range(KT)]


def order():
    o = Order()

    def emit(steps):
        for s in steps:
            if s[0] == "item":
                for g in groups(s[1], s[2]):
                    o.group(*s[1:], g)
            elif s[0] == "drain":
                o.drain()
            else:
                o.append(s)

    emit([("ctxk", l, f) for l in range(2) for f in range(KT)])
    emit([("ctxv", l, b) for l in range(2) for b in range(B)])
    for c in range(NCHUNK):
        emit(prologue(c) + self_q(c))
        emit(maxes("sa", c, 0))
        for hg in range(NHG):
            if hg + 1 < NHG:
                emit(maxes("sa", c, hg + 1))
            emit([("item", "sa", c, hg)])
        emit([("drain",)])
        emit(post(c))
    return list(o)


def build(nc, x, ctxT, sq, fcw, cols, rows, lnrow, ident, masks, trig, out):
    ORDER = order()
    nth, seen = {}, {}
    for s in ORDER:
        seen[s[0]] = seen.get(s[0], 0) + 1
        assert s not in nth, s
        nth[s] = seen[s[0]]
    chain_use, misc_use = {}, {}
    for s in ORDER:
        if s[0] in ("ctxk", "ctxv", "tr", "proj", "v", "wo"):
            chain_use[s] = len(chain_use)
        if s[0] == "down" and s[3] == 0:
            for g in range(NT // 2):
                chain_use[("res", s[1], s[2], g)] = len(chain_use)
        if s[0] in ("row", "turn", "up"):
            misc_use[s] = len(misc_use)
    with ExitStack() as ctx:
        def sb(name, shape, dt=F32):
            return ctx.enter_context(nc.sbuf_tensor(name, shape, dt))

        def psum(name):
            return ctx.enter_context(nc.psum_tensor(name, [P, 512], F32))

        def sem(name):
            return ctx.enter_context(nc.semaphore(name))

        w_sq = {n: sb("w_" + n, [P, KT, E]) for n in ("sa_wq", "sa_wk", "sa_wv", "sa_wo", "ca_wq", "ca_wo", "l1_wq")}
        w_up = [sb(f"w_up{l}", [P, KT, FF]) for l in range(2)]
        w_down = [sb(f"w_down{l}", [P, NM, E]) for l in range(2)]
        col = sb("col", [P, NCOLS])
        g4b4 = sb("g4b4", [P, 2, E])
        idf = sb("idf", [P, P])
        idb = sb("idb", [P, P], BF16)
        mask = sb("mask", [P, MASKW], BF16)
        maskw, maskt, maskb = mask[:, 0:2 * P], mask[:, 2 * P:3 * P], mask[:, 3 * P:5 * P]
        cosT = sb("cosT", [P, LX])
        sinT = sb("sinT", [P, LX])
        ones3 = sb("ones3", [3, P], BF16)
        bias3 = sb("bias3", [3, len(BIAS_ROWS), E], BF16)

        KA = sb("KA", [SROW + 2, 2, H, CH], BF16)
        QA = sb("QA", [SROW + 2, H, CH], BF16)
        QC = sb("QC", [SROW + 2, HH, CH], BF16)
        KC = sb("KC", [SROW + 2, 2, H, B, LYP], BF16)
        V = sb("V", [P, 2, NT, H, HD + 1])
        VA = sb("VA", [P, 2, B, H, HD + 1])
        VB = sb("VB", [P, 2, B, NHG, HD + 1])
        probs = sb("probs", [P, 2, HG, CH])
        mcol = sb("mcol", [P, NROW, 2, HG, NT])
        mrow = sb("mrow", [HG * NT, NROW, 2, P], BF16)
        osb = sb("osb", [P, 2, CH])
        rec = sb("rec", [P, 2, NT, HG])
        a_sa = sb("a_sa", [P, NT, E])
        a_ctx = sb("a_ctx", [P, NT, E])

        xb = sb("xb", [P, 2, NT, E])
        xn = sb("xn", [P, NT, E])
        hT = sb("hT", [P, 2, KT, CH])
        hid = sb("hid", [P, 2, CH])
        rot = sb("rot", [P, 2, CH])
        rest = sb("rest", [P, 2, CH])
        part = sb("part", [P, 2, 3, CH], BF16)
        st6 = sb("st6", [P, NT, 6])
        mv = sb("mv", [P, NT, 2])
        nw = sb("nw", [P, 5, NT])

        w_ctx = probs[:, 0, :, :].rearrange("p a b -> p (a b)").rearrange("p (n k e) -> p n k e", n=4, k=KT)
        cT = osb[:, :, 0:B * LY]
        maskf = rot[:, :, :].rearrange("p a b -> p (a b)")[:, 0:MASKW]
        NB = len(BIAS_ROWS) * E
        brow = probs[0:1, 1, :, :].rearrange("p a b -> p (a b)")[:, 0:NB]
        bpart = [hid[0:1, :, :].rearrange("p a b -> p (a b)").bitcast(BF16)[:, 0:NB]]
        bpart += [hT[0:1, i, :, :].rearrange("p a b -> p (a b)").bitcast(BF16)[:, 0:NB] for i in range(2)]

        ps_max = [psum(f"ps_max{i}") for i in range(2)]
        ps_exp = [psum(f"ps_exp{i}") for i in range(2)]
        ps_o = psum("ps_o")
        ps_misc = psum("ps_misc")
        ps_chain = [psum(f"ps_chain{i}") for i in range(2)]

        s_const, s_cols, s_mask_in, s_rows_in = sem("const_in"), sem("cols_in"), sem("mask_in"), sem("rows_in")
        s_wctx, s_wqkv, s_wrest = sem("wctx_in"), sem("wqkv_in"), sem("wrest_in")
        s_x = [sem(f"x_in{i}") for i in range(2)]
        s_stored = [sem(f"stored{i}") for i in range(2)]
        s_ones = sem("ones_set")
        s_mask = sem("mask_ready")
        s_bpart, s_bmove = sem("bias_parts_ready"), sem("bias_parts_moved")
        s_chain_ready = sem("chain_ready")
        s_chain_free = [sem(f"chain_read{i}") for i in range(2)]
        s_misc_ready, s_misc_free = sem("misc_ready"), sem("misc_read")
        s_max_ready, s_max_done = sem("max_ready"), sem("max_done")
        s_both = sem("two_halves_max")
        s_exp_ready, s_exp_done = sem("exp_ready"), sem("exp_done")
        s_pv, s_evac = sem("pv_done"), sem("o_evacuated")
        s_mput = [sem(f"mrow_placed{i}") for i in range(NROW)]
        s_xn = sem("xn_ready")
        s_p1, s_p3 = sem("part1_ready"), sem("parts_ready")
        s_put = {k: [sem(f"placed_{k}{f}") for f in range(KT)] for k in ("qs", "ks", "qc", "kc")}
        s_down = sem("down_done")
        s_scaled = sem("q_weights_scaled")
        s_add, s_lnout = sem("attention_added"), sem("ln4_written")
        s_dve, s_pool = sem("dve_chain"), sem("pool_chain")
        block = ctx.enter_context(nc.Block())

        def c0(name, i=0):
            return col[:, COLS[name][0] + i:COLS[name][0] + i + 1]

        def after_chain(eng, s):
            eng.wait_ge(s_chain_free[chain_use[s] % 2], chain_use[s] // 2 + 1)

        def after_misc(eng, s):
            eng.wait_ge(s_misc_free, misc_use[s] + 1)

        def operand(s):
            if s[0] == "ctxk":
                return "kc", s[2]
            return (s[1] if s[1] in ("qs", "ks") else "qc"), s[3]

        proj_nth, put_nth, item_nth, both_nth, grp_end, put_count, n_exps = {}, {}, {}, {}, {}, {}, 0
        for s in ORDER:
            if s[0] in ("proj", "ctxk"):
                proj_nth[s] = len(proj_nth) + 1
                put_count[operand(s)] = put_count.get(operand(s), 0) + 1
                put_nth[s] = put_count[operand(s)]
            elif s[0] == "row":
                item_nth[s[1:]] = len(item_nth) + 1
                if s[1] == "sa" and s[2] % 2:
                    both_nth[s[1:]] = len(both_nth) + 1
            elif s[0] == "exp":
                n_exps += 1 if s[4] == "B" else HG
                grp_end[s[1:]] = n_exps
        projs = sorted(proj_nth, key=proj_nth.get)

        def placed(eng, s):
            key, f = operand(s)
            eng.wait_ge(s_put[key][f], 16 * NPROD * (B if key == "kc" else 1) * put_nth[s])

        @block.sync
        def _(sp):
            sp.dma_start(idf[:, :], ident).then_inc(s_const, 16)
            sp.dma_start(cosT[:, :], trig[0]).then_inc(s_const, 16)
            sp.dma_start(sinT[:, :], trig[1]).then_inc(s_const, 16)
            sp.dma_start(col[:, :], cols).then_inc(s_cols, 16)
            sp.dma_start(cT, ctxT).then_inc(s_wctx, 16)
            for i, n in enumerate(("ca_wk", "ca_wv", "l1_wk", "l1_wv")):
                sp.dma_start(w_ctx[:, i], sq[n]).then_inc(s_wctx, 16)
            sp.dma_start(maskf, masks).then_inc(s_mask_in, 16)
            sp.dma_start(brow, rows).then_inc(s_rows_in, 16)
            for n in ("sa_wk", "sa_wv", "sa_wq"):
                sp.dma_start(w_sq[n][:, :, :], sq[n]).then_inc(s_wqkv, 16)
            def load(c):
                src = x[c // 2, (c % 2) * CH:(c % 2 + 1) * CH, :].rearrange("(t p) e -> p t e", p=P)
                sp.dma_start(xb[:, c % 2, :, :], src).then_inc(s_x[c % 2], 16)

            load(0)
            for n in ("sa_wo", "ca_wq", "ca_wo", "l1_wq"):
                sp.dma_start(w_sq[n][:, :, :], sq[n]).then_inc(s_wrest, 16)
            for l in range(2):
                sp.dma_start(w_up[l][:, :, :], fcw[2 * l]).then_inc(s_wrest, 16)
                sp.dma_start(w_down[l][:, :, :], fcw[2 * l + 1]).then_inc(s_wrest, 16)
            sp.dma_start(g4b4[:, :, :], lnrow).then_inc(s_wrest, 16)
            sp.wait_ge(s_bpart, 3)
            for i in range(3):
                sp.dma_start(bias3[i:i + 1, :, :], bpart[i]).then_inc(s_bmove, 16)
            for s in ORDER:
                k = s[0]
                if k == "load" and s[1] > 0:
                    c = s[1]
                    if c >= 2:
                        sp.wait_ge(s_stored[c % 2], 16 * (c // 2))
                    load(c)
                elif k in ("proj", "ctxk"):
                    i = proj_nth[s] % 2
                    sp.wait_ge(s_p3, proj_nth[s])
                    if k == "ctxk":
                        _, l, f = s
                        for g in range(NPROD):
                            for b in range(B):
                                sp.dma_start(KC[g * HD:(g + 1) * HD, l, f * HH:(f + 1) * HH, b, 0:LY],
                                             part[:, i, KPART[g], b * LY:(b + 1) * LY]).then_inc(s_put["kc"][f], 16)
                    else:
                        _, kind, c, f = s
                        key = operand(s)[0]
                        dst = {"qs": QA[:, f * HH:(f + 1) * HH, :], "ks": KA[:, c % 2, f * HH:(f + 1) * HH, :],
                               "qc": QC[:, :, :]}[key]
                        which = KPART if kind == "ks" else QPART
                        for g in range(NPROD):
                            sp.dma_start(dst[g * HD:(g + 1) * HD, :, :],
                                         part[:, i, which[g], :]).then_inc(s_put[key][f], 16)
                elif k == "row":
                    _, att, c, hg = s
                    n = item_nth[s[1:]]
                    after_misc(sp, s)
                    q, h0 = (QA, hg * HG) if att == "sa" else (QC, (hg % 2) * HG)
                    for i in range(2):
                        sp.dma_start(q[SROW + i:SROW + i + 1, h0:h0 + HG, :],
                                     mrow[:, n % NROW, i, :]).then_inc(s_mput[n % NROW], 16)
                elif k == "store":
                    c = s[1]
                    for g in range(NT // 2):
                        after_chain(sp, ("res", 1, c, g))
                    dst = out[c // 2, (c % 2) * CH:(c % 2 + 1) * CH, :].rearrange("(t p) e -> p t e", p=P)
                    sp.dma_start(dst, xb[:, c % 2, :, :]).then_inc(s_stored[c % 2], 16)
            for i in range(2):
                sp.wait_ge(s_stored[i], 16 * (NCHUNK // 2))

        @block.tensor
        def _(pe):
            pe.wait_ge(s_const, 48)
            pe.wait_ge(s_wctx, 80)
            n_max = [0]
            n_exp = [0]

            def chain_bank(s):
                n = chain_use[s]
                if n >= 2:
                    pe.wait_ge(s_chain_free[n % 2], n // 2)
                return ps_chain[n % 2]

            def misc_bank(s):
                n = misc_use[s]
                if n >= 1:
                    pe.wait_ge(s_misc_free, n)
                return ps_misc

            def add_bias(dst, name, m=P, start=True):
                i = BIAS_ROWS.index(name)
                pe.matmul(dst, ones3[0:3, 0:m], bias3[0:3, i, :], start=start, stop=False, skip_group_check=True)

            waited = set()

            def once(key, s, v):
                if key not in waited:
                    waited.add(key)
                    pe.wait_ge(s, v)

            for s in ORDER:
                k = s[0]
                if k == "ctxk":
                    _, l, f = s
                    bank = chain_bank(s)
                    for t in range(KT):
                        mm = pe.matmul(bank[:, 0:B * LY], w_ctx[:, 2 * l, t, f * P:(f + 1) * P], cT[:, t, :],
                                       start=(t == 0), stop=(t == KT - 1))
                    mm.then_inc(s_chain_ready, 1)
                elif k == "ctxv":
                    _, l, b = s
                    once("bias", s_bmove, 48)
                    once("ones", s_ones, 6)
                    bank = chain_bank(s)
                    name = ("ca_bv", "l1_bv")[l]
                    add_bias(bank[:, 0:E], name)
                    for t in range(KT):
                        pe.matmul(bank[:, 0:E], cT[:, t, b * LY:b * LY + P], w_ctx[:, 2 * l + 1, t, :],
                                  start=False, stop=(t == KT - 1), skip_group_check=True)
                    for j in range(HG):
                        dst = bank[32 * j:32 * j + LYB, E:2 * E]
                        add_bias(dst, name, LYB, start=False)
                        for t in range(KT):
                            mm = pe.matmul(dst, cT[:, t, b * LY + P:(b + 1) * LY], w_ctx[:, 2 * l + 1, t, :],
                                           start=False, stop=(t == KT - 1), skip_group_check=True)
                    mm.then_inc(s_chain_ready, 1)
                elif k == "tr":
                    _, what, c, f = s
                    if what in ("ln1", "ln2", "ln3", "ln4"):
                        pe.wait_ge(s_xn, nth[("stats", what, c)])
                        src = xn
                    elif what == "x3":
                        for g in range(NT // 2):
                            after_chain(pe, ("res", 0, c, g))
                        src = xb[:, c % 2]
                    else:
                        att = what[3:]
                        after_misc(pe, ("turn", att, c, NHG - 1))
                        src = a_sa if att == "sa" else a_ctx
                    bank = chain_bank(s)
                    for t in range(NT):
                        mm = pe.transpose(bank[:, t * P:(t + 1) * P], src[:, t, f * P:(f + 1) * P], idf[:, :])
                    mm.then_inc(s_chain_ready, 1)
                elif k in ("proj", "v", "wo"):
                    what = "ln1" if k == "v" or (k == "proj" and s[1] in ("qs", "ks")) else None
                    if k == "v":
                        name, c = "sa_wv", s[1]
                    elif k == "wo":
                        name, c = s[1] + "_wo", s[2]
                        what = "oT_" + s[1]
                    else:
                        name, c = {"qs": "sa_wq", "ks": "sa_wk", "qca": "ca_wq", "qla": "l1_wq"}[s[1]], s[2]
                        what = what or {"qca": "ln2", "qla": "x3"}[s[1]]
                    once("wqkv", s_wqkv, 48)
                    if what != "ln1":
                        once("wrest", s_wrest, 16 * 9)
                    after_chain(pe, ("tr", what, c, KT - 1))
                    src = hT[:, 0 if what == "ln1" else 1]
                    w = w_sq[name]
                    if name.endswith("_wq"):
                        once(name, s_scaled, {"sa_wq": 4, "ca_wq": 5, "l1_wq": 6}[name])
                    bank = chain_bank(s)
                    if k == "proj":
                        f = s[3]
                        for t in range(KT):
                            mm = pe.matmul(bank[:, :], w[:, t, f * P:(f + 1) * P], src[:, t, :],
                                           start=(t == 0), stop=(t == KT - 1))
                    else:
                        for i in range(2):
                            dst = bank[:, i * E:(i + 1) * E]
                            add_bias(dst, "sa_bv" if k == "v" else s[1] + "_bo")
                            tok = (2 * s[-1] + i) * P
                            for t in range(KT):
                                mm = pe.matmul(dst, src[:, t, tok:tok + P], w[:, t, :],
                                               start=False, stop=(t == KT - 1), skip_group_check=True)
                    mm.then_inc(s_chain_ready, 1)
                elif k == "up":
                    _, l, c, m = s
                    after_chain(pe, ("tr", ("ln3", "ln4")[l], c, KT - 1))
                    bank = misc_bank(s)
                    for t in range(KT):
                        mm = pe.matmul(bank[:, :], w_up[l][:, t, m * P:(m + 1) * P], hT[:, 1, t, :],
                                       start=(t == 0), stop=(t == KT - 1))
                    mm.then_inc(s_misc_ready, 1)
                elif k == "down":
                    _, l, c, m = s
                    banks = []
                    for g in range(NT // 2):
                        use = ("res", l, c, g)
                        banks.append(chain_bank(use) if m == 0 else ps_chain[chain_use[use] % 2])
                    after_misc(pe, ("up", l, c, m))
                    for t in range(NT):
                        dst = banks[t // 2][:, (t % 2) * E:(t % 2 + 1) * E]
                        if m == 0:
                            add_bias(dst, ("fc2_b", "l1_b2")[l], start=(t % 2 == 0))
                        mm = pe.matmul(dst, hid[:, m % 2, t * P:(t + 1) * P], w_down[l][:, m, :],
                                       start=False, stop=(m == NM - 1), skip_group_check=True)
                        if m == NM - 1 and t % 2:
                            mm.then_inc(s_chain_ready, 1)
                        elif t == NT - 1:
                            mm.then_inc(s_down, 1)
                elif k == "max":
                    _, att, c, hg, u = s
                    unit = units(att, c)[u]
                    once("mask", s_mask, 2)
                    once("ones", s_ones, 6)
                    if u == 0:
                        f = hg // 2
                        if att == "sa":
                            placed(pe, ("proj", "qs", c, f))
                            placed(pe, ("proj", "ks", c, f))
                        else:
                            placed(pe, ("proj", "q" + att, c, f))
                            once(("kc", f), s_put["kc"][f], 16 * NPROD * B * 2)
                    if n_max[0] >= 2:
                        pe.wait_ge(s_max_done, n_max[0] - 1)
                    bank = ps_max[n_max[0] % 2]
                    n_max[0] += 1
                    for t, h, half, n, pt, at0 in unit:
                        dst = bank[:, at0:at0 + n]
                        if att == "sa":
                            q = QA[0:SROW, hg * HG + h, t * P:(t + 1) * P]
                            kk = KA[0:SROW, half, hg * HG + h, 0:n]
                            causal = [(n - P, P, maskw[:, 0:P])] if pt == 0 else []
                        else:
                            l = int(att == "la")
                            q = QC[0:SROW, (hg % 2) * HG + h, t * P:(t + 1) * P]
                            kk = KC[0:SROW, l, hg * HG + h, c // 2, 0:LY]
                            causal = []
                            if l and c % 2 == 0 and t < 2:
                                causal = [[(0, LY, maskw[:, 0:LY])], [(P, LYB, maskw[:, 0:LYB])]][t]
                        mm = pe.matmul(dst, q, kk, start=True, stop=not causal)
                        for a0, w0, mk in causal:
                            mm = pe.matmul(bank[:, at0 + a0:at0 + a0 + w0], idb[:, :], mk, start=False, stop=True)
                    mm.then_inc(s_max_ready, 1)
                elif k == "row":
                    n = item_nth[s[1:]]
                    _, att, c, hg = s
                    if s[1:] in both_nth:
                        pe.wait_ge(s_both, both_nth[s[1:]])
                    else:
                        pe.wait_ge(s_max_done, nth[("max", att, c, hg, len(units(att, c)) - 1)])
                    bank = misc_bank(s)
                    src = mcol[:, n % NROW, 0, :, :].rearrange("p h t -> p (h t)")
                    pe.transpose(bank[0:NT * HG, 0:P], src, idf[:, :]).then_inc(s_misc_ready, 1)
                elif k == "exp":
                    _, att, c, hg, g = s
                    if g == groups(att, c)[0]:
                        n = item_nth[(att, c, hg)]
                        pe.wait_ge(s_mput[n % NROW], 32 * ((n - 1) // NROW + 1))
                    l = int(att == "la")
                    for h in range(HG):
                        hh = hg * HG + h
                        if g == "B" and h:
                            pass
                        else:
                            if n_exp[0] >= 2:
                                pe.wait_ge(s_exp_done, n_exp[0] - 1)
                            bank = ps_exp[n_exp[0] % 2]
                            n_exp[0] += 1
                        if att == "sa":
                            r = g - NT * (c % 2)
                            q0 = max(r, 0) * P
                            mm = pe.matmul(bank[:, q0:CH], KA[:, g // NT, hh, (g % NT) * P:(g % NT + 1) * P],
                                           QA[:, hh, q0:CH], start=True, stop=(r < 0))
                            if r >= 0:
                                mm = pe.matmul(bank[:, q0:q0 + P], idb[:, :], maskt, start=False, stop=True)
                            mm.then_inc(s_exp_ready, 1)
                        elif g == "A":
                            causal = l and c % 2 == 0
                            q = QC[:, (hg % 2) * HG + h, :]
                            mm = pe.matmul(bank[:, :], KC[:, l, hh, c // 2, 0:P], q, start=True, stop=not causal)
                            if causal:
                                mm = pe.matmul(bank[:, 0:P], idb[:, :], maskt, start=False, stop=True)
                            mm.then_inc(s_exp_ready, 1)
                        else:
                            causal = l and c % 2 == 0
                            q = QC[:, (hg % 2) * HG + h, :]
                            mm = pe.matmul(bank[32 * h:32 * h + 32, :], KC[:, l, hh, c // 2, P:LYP], q,
                                           start=True, stop=not causal, skip_group_check=True)
                            if h == HG - 1:
                                if causal:
                                    mm = pe.matmul(bank[:, 0:2 * P], idb[:, :], maskb, start=False, stop=True,
                                                   skip_group_check=True)
                                mm.then_inc(s_exp_ready, 1)
                elif k == "pv":
                    _, att, c, hg, g = s
                    n = nth[s]
                    pe.wait_ge(s_exp_done, grp_end[(att, c, hg, g)])
                    first = g == groups(att, c)[0]
                    last = g == groups(att, c)[-1]
                    if first:
                        item = nth[("evac", att, c, hg)]
                        if item > 1:
                            pe.wait_ge(s_evac, item - 1)
                        if att == "sa":
                            for i in range(NT // 2):
                                after_chain(pe, ("v", c, i))
                    for h in range(HG):
                        hh = hg * HG + h
                        p0, q0 = 32 * h, 0
                        if att == "sa":
                            q0 = max(g - NT * (c % 2), 0) * P
                            v, pr = V[:, g // NT, g % NT, hh, :], probs[:, n % 2, h, q0:CH]
                        elif g == "A":
                            v, pr = VA[:, int(att == "la"), c // 2, hh, :], probs[:, n % 2, h, :]
                        else:
                            v = VB[p0:p0 + LYB, int(att == "la"), c // 2, hg, :]
                            pr = probs[p0:p0 + LYB, n % 2, 0, :]
                        mm = pe.matmul(ps_o[p0:p0 + HD + 1, q0:CH], v, pr, start=first, stop=last,
                                       skip_group_check=True)
                    mm.then_inc(s_pv, 1)
                elif k == "turn":
                    n = nth[s]
                    pe.wait_ge(s_evac, n)
                    bank = misc_bank(s)
                    for t in range(NT):
                        mm = pe.transpose(bank[:, t * P:(t + 1) * P], osb[:, n % 2, t * P:(t + 1) * P], idf[:, :])
                    mm.then_inc(s_misc_ready, 1)

        @block.vector
        def _(dve):
            chain = [0]

            def link(ins):
                chain[0] += 1
                ins.then_inc(s_dve, 1)
                dve.wait_ge(s_dve, chain[0])

            dve.memset(ps_o[:, :], 0.0)
            dve.memset(KA[SROW:SROW + 2, :, :, :], 1.0).then_inc(s_ones, 1)
            dve.memset(KC[:, :, :, :, LY:LYP], 0.0).then_inc(s_ones, 1)
            dve.memset(KC[SROW:SROW + 2, :, :, :, 0:LY], 1.0).then_inc(s_ones, 1)
            dve.memset(ones3[:, :], 1.0).then_inc(s_ones, 1)
            dve.memset(V[:, :, :, :, HD:HD + 1], 1.0).then_inc(s_ones, 1)
            dve.memset(VA[:, :, :, :, HD:HD + 1], 1.0)
            dve.memset(VB[:, :, :, :, HD:HD + 1], 1.0).then_inc(s_ones, 1)
            dve.wait_ge(s_mask_in, 16)
            dve.tensor_copy(mask[:, :], maskf).then_inc(s_mask, 1)
            dve.wait_ge(s_const, 48)
            dve.tensor_copy(idb[:, :], idf[:, :]).then_inc(s_mask, 1)
            dve.wait_ge(s_rows_in, 16)
            for i in range(3):
                dve.tensor_copy(bpart[i], brow).then_inc(s_bpart, 1)
                if i < 2:
                    dve.wait_ge(s_bpart, i + 1)
                    link(dve.tensor_tensor(brow, brow, bpart[i], ALU.subtract))
            dve.wait_ge(s_scaled, 3)
            stats = [s for s in ORDER if s[0] == "stats"]
            for s in ORDER:
                k = s[0]
                if k in ("ctxk", "proj"):
                    n = proj_nth[s]
                    u = chain_use[s]
                    i = n % 2
                    bank = ps_chain[u % 2]
                    if k == "ctxk":
                        rope, name, f = s[1] == 0, ("ca_bk", "l1_bk")[s[1]], s[2]
                        pieces = [(b * LY, 0, LY) for b in range(B)]
                        width = B * LY
                    else:
                        kind, c, f = s[1:]
                        rope, name = kind != "qla", {"qs": "sa_bq", "ks": "sa_bk", "qca": "ca_bq", "qla": "l1_bq"}[kind]
                        pieces = [(0, (c % 2) * CH, CH)]
                        width = CH
                    if n > 2:
                        placed(dve, projs[n - 3])
                    dve.wait_ge(s_chain_ready, u + 1)
                    r, w = rot[:, i, 0:width], rest[:, i, 0:width]
                    bc = c0(name, f)
                    if rope:
                        for a0, t0, wd in pieces:
                            for lo, hi in ((0, 64), (64, 0)):
                                dve.scalar_tensor_tensor(w[lo:lo + 64, a0:a0 + wd], bank[hi:hi + 64, a0:a0 + wd],
                                                         bc[hi:hi + 64], sinT[hi:hi + 64, t0:t0 + wd], ALU.add, ALU.mult)
                            ins = dve.scalar_tensor_tensor(r[:, a0:a0 + wd], bank[:, a0:a0 + wd], bc,
                                                           cosT[:, t0:t0 + wd], ALU.add, ALU.mult)
                        ins.then_inc(s_chain_free[u % 2], 1)
                        after_chain(dve, s)
                        link(dve.tensor_tensor(r, r, w, ALU.add))
                        dve.tensor_copy(part[:, i, 0, 0:width], r).then_inc(s_p1, 1)
                    else:
                        ins = dve.tensor_scalar(r, bank[:, 0:width], bc, None, ALU.add)
                        ins.then_inc(s_chain_free[u % 2], 1)
                        after_chain(dve, s)
                        dve.tensor_copy(part[:, i, 0, 0:width], r).then_inc(s_p1, 1)
                elif k == "wo" or k == "res":
                    c = s[2]
                    u = chain_use[s]
                    g = s[3]
                    dve.wait_ge(s_chain_ready, u + 1)
                    if k == "res" and s[1] == 1:
                        dve.wait_ge(s_lnout, c + 1)
                    xs = xb[:, c % 2, 2 * g:2 * g + 2, :].rearrange("p t e -> p (t e)")
                    dve.tensor_tensor(xs, xs, ps_chain[u % 2][:, :], ALU.add).then_inc(s_chain_free[u % 2], 1)
                elif k == "stats":
                    _, what, c = s
                    if what == "ln1":
                        dve.wait_ge(s_x[c % 2], 16 * (c // 2 + 1))
                    elif what == "ln4":
                        dve.wait_ge(s_add, c + 1)
                    else:
                        for g in range(NT // 2):
                            after_chain(dve, ("wo", {"ln2": "sa", "ln3": "ca"}[what], c, g))
                    for t in range(NT):
                        ins = dve.bn_stats(st6[:, t, :], xb[:, c % 2, t, :])
                    link(ins)
                    for t in range(NT):
                        ins = dve.bn_aggr(mv[:, t, :], st6[:, t, :])
                    link(ins)
                    v, y, t1, t2 = nw[:, 0], nw[:, 1], nw[:, 2], nw[:, 3]
                    link(dve.tensor_scalar(v, mv[:, :, 1], EPS, None, ALU.add))
                    link(dve.tensor_scalar(t1.bitcast(I32), v.bitcast(I32), 1, None, ALU.logical_shift_right))
                    link(dve.tensor_scalar(y.bitcast(I32), t1.bitcast(I32), -1, RSQRT_GUESS, ALU.mult, ALU.add))
                    for _ in range(3):
                        link(dve.tensor_tensor(t1, y, y, ALU.mult))
                        link(dve.scalar_tensor_tensor(t2, t1, -0.5, v, ALU.mult, ALU.mult))
                        link(dve.scalar_tensor_tensor(y, t2, 1.5, y, ALU.add, ALU.mult))
                    if nth[s] > 1:
                        prev = stats[nth[s] - 2]
                        dve.wait_ge(s_chain_ready, chain_use[("tr", *prev[1:], KT - 1)] + 1)
                        if prev[1] == "ln4":
                            dve.wait_ge(s_lnout, prev[2] + 1)
                    for t in range(NT):
                        ins = dve.tensor_scalar(xn[:, t, :], xb[:, c % 2, t, :], mv[:, t, 0:1], y[:, t:t + 1],
                                                ALU.subtract, ALU.mult)
                    ins.then_inc(s_xn, 1)
                elif k == "max":
                    _, att, c, hg, u = s
                    unit = units(att, c)[u]
                    n = item_nth[(att, c, hg)]
                    dve.wait_ge(s_max_ready, nth[s])
                    bank = ps_max[(nth[s] - 1) % 2]
                    t, h, _, w, pt, _ = unit[0]
                    step = w if att == "sa" else LYP
                    src = bank[:, 0:len(unit) * step].rearrange("p (n w) -> p n w", w=step)[:, :, 0:w]
                    if att == "sa":
                        dst = mcol[:, n % NROW, pt, h:h + len(unit), t]
                    else:
                        k0 = h * NT + t
                        dst = mcol[:, n % NROW, 0, :, :].rearrange("p h t -> p (h t)")[:, k0:k0 + len(unit)]
                    dve.tensor_reduce(dst, src, AX.X, ALU.max).then_inc(s_max_done, 1)
                elif k == "row":
                    _, att, c, hg = s
                    n = item_nth[s[1:]]
                    if s[1:] in both_nth:
                        dve.wait_ge(s_max_done, nth[("max", att, c, hg, len(units(att, c)) - 1)])
                        m0, m1 = mcol[:, n % NROW, 0, :, :], mcol[:, n % NROW, 1, :, :]
                        dve.tensor_tensor(m0, m0, m1, ALU.max).then_inc(s_both, 1)
                    dve.wait_ge(s_misc_ready, misc_use[s] + 1)
                    src = ps_misc[0:NT * HG, 0:P]
                    link(dve.tensor_scalar(mrow[:, n % NROW, 0, :], src, -1.0, None, ALU.mult))
                    dve.scalar_tensor_tensor(mrow[:, n % NROW, 1, :], src, -1.0, mrow[:, n % NROW, 0, :],
                                             ALU.mult, ALU.subtract).then_inc(s_misc_free, 1)
                elif k == "turn":
                    _, att, c, hg = s
                    n = nth[s]
                    if att == "ca" and c > 0 and hg == 0:
                        dve.wait_ge(s_add, c)
                    dve.wait_ge(s_misc_ready, misc_use[s] + 1)
                    src = ps_misc[:, :].rearrange("p (t h w) -> p t h w", t=NT, h=HG)
                    r = rec[:, n % 2]
                    link(dve.reciprocal(r, src[:, :, :, HD]))
                    dst = (a_sa if att == "sa" else a_ctx)[:, :, hg * HG * HD:(hg + 1) * HG * HD]
                    dst = dst.rearrange("p t (h d) -> p t h d", h=HG)
                    rb = r.unsqueeze(3).to_broadcast([P, NT, HG, HD])
                    dve.tensor_tensor(dst, src[:, :, :, 0:HD], rb, ALU.mult).then_inc(s_misc_free, 1)

        @block.scalar
        def _(act):
            act.wait_ge(s_cols, 16)
            n_exp = 0
            for s in ORDER:
                k = s[0]
                if k in ("tr", "v", "ctxv"):
                    u = chain_use[s]
                    act.wait_ge(s_chain_ready, u + 1)
                    bank = ps_chain[u % 2]
                if k == "tr":
                    _, what, c, f = s
                    dst = hT[:, 0 if what == "ln1" else 1, f, :]
                    if what[:2] == "ln":
                        ins = act.activation(dst, bank[:, :], ACT.Identity, bias=c0(what + "_b", f), scale=c0(what + "_g", f))
                    else:
                        ins = act.activation(dst, bank[:, :], ACT.Copy)
                    ins.then_inc(s_chain_free[u % 2], 1)
                elif k == "v":
                    _, c, g = s
                    act.activation(V[:, c % 2, 2 * g:2 * g + 2, :, 0:HD],
                                   bank[:, :].rearrange("p (t h d) -> p t h d", t=2, h=H),
                                   ACT.Copy).then_inc(s_chain_free[u % 2], 1)
                elif k == "ctxv":
                    _, l, b = s
                    act.activation(VA[:, l, b, :, 0:HD], bank[:, 0:E].rearrange("p (h d) -> p h d", h=H), ACT.Copy)
                    for j in range(HG):
                        q = slice(32 * j, 32 * j + LYB)
                        src = bank[q, E:2 * E].rearrange("p (g h d) -> p g h d", g=NHG, h=HG)[:, :, j, :]
                        ins = act.activation(VB[q, l, b, :, 0:HD], src, ACT.Copy)
                    ins.then_inc(s_chain_free[u % 2], 1)
                elif k == "up":
                    _, l, c, m = s
                    act.wait_ge(s_misc_ready, misc_use[s] + 1)
                    act.activation(hid[:, m % 2, :], ps_misc[:, :], (ACT.Gelu_apprx_tanh, ACT.Gelu)[l],
                                   bias=c0(("fc1_b", "l1_b1")[l], m)).then_inc(s_misc_free, 1)
                elif k == "exp":
                    _, att, c, hg, g = s
                    n = nth[s]
                    if n > 2:
                        act.wait_ge(s_pv, n - 2)
                    for h in range(1 if g == "B" else HG):
                        n_exp += 1
                        q0 = max(g - NT * (c % 2), 0) * P if att == "sa" else 0
                        act.wait_ge(s_exp_ready, n_exp)
                        act.activation(probs[:, n % 2, h, q0:CH], ps_exp[(n_exp - 1) % 2][:, q0:CH],
                                       ACT.Exp).then_inc(s_exp_done, 1)
                elif k == "evac":
                    _, att, c, hg = s
                    act.wait_ge(s_pv, nth[("pv", att, c, hg, groups(att, c)[-1])])
                    act.activation(osb[:, nth[s] % 2, :], ps_o[:, :], ACT.Copy).then_inc(s_evac, 1)

        @block.gpsimd
        def _(pool):
            pool.wait_ge(s_cols, 16)
            for name in ("sa_bq", "ca_bq", "l1_bq"):
                b = col[:, COLS[name][0]:COLS[name][0] + KT]
                pool.tensor_scalar(b, b, SCALE, None, ALU.mult).then_inc(s_scaled, 1)

            def scale(name):
                w = w_sq[name][:, :, :]
                pool.tensor_scalar(w, w, SCALE, None, ALU.mult).then_inc(s_scaled, 1)

            pool.wait_ge(s_wqkv, 48)
            scale("sa_wq")
            chain = 0
            for s in ORDER:
                k = s[0]
                if s == ("v", 0, 0):
                    pool.wait_ge(s_wrest, 16 * 9)
                    scale("ca_wq")
                    scale("l1_wq")
                if k in ("proj", "ctxk"):
                    n = proj_nth[s]
                    width = B * LY if k == "ctxk" else CH
                    r, w = rot[:, n % 2, 0:width], rest[:, n % 2, 0:width]
                    p1, p2, p3 = (part[:, n % 2, i, 0:width] for i in range(3))
                    pool.wait_ge(s_p1, n)
                    chain += 1
                    pool.tensor_tensor(w, r, p1, ALU.subtract).then_inc(s_pool, 1)
                    pool.wait_ge(s_pool, chain)
                    chain += 1
                    pool.tensor_copy(p2, w).then_inc(s_pool, 1)
                    pool.wait_ge(s_pool, chain)
                    pool.tensor_tensor(p3, w, p2, ALU.subtract).then_inc(s_p3, 1)
                elif k == "addatt":
                    c = s[1]
                    after_misc(pool, ("turn", "la", c, NHG - 1))
                    xs = xb[:, c % 2, :, :]
                    pool.tensor_tensor(xs, xs, a_ctx[:, :, :], ALU.add).then_inc(s_add, 1)
                elif k == "lnout":
                    c = s[1]
                    pool.wait_ge(s_xn, nth[("stats", "ln4", c)])
                    pool.wait_ge(s_wrest, 16 * 9)
                    for t in range(NT):
                        chain += 1
                        pool.tensor_tensor(xb[:, c % 2, t, :], xn[:, t, :], g4b4[:, 0, :], ALU.mult).then_inc(s_pool, 1)
                    pool.wait_ge(s_pool, chain)
                    for t in range(NT):
                        ins = pool.tensor_tensor(xb[:, c % 2, t, :], xb[:, c % 2, t, :], g4b4[:, 1, :], ALU.add)
                    ins.then_inc(s_lnout, 1)


def rows_first(a):
    return np.ascontiguousarray(a.reshape(-1, P, a.shape[1]).transpose(1, 0, 2))


def by_head(a):
    return a.reshape(a.shape[:-1] + (KT, HH, HD)).swapaxes(-1, -2).reshape(a.shape)


def constants():
    q, k = np.arange(P)[:, None], np.arange(2 * P)[None, :]
    first = np.where(k > q, NEG, 0.0)
    second = np.where(q > k[:, :P], NEG, 0.0)
    last = np.where(P + q % 32 > k, NEG, 0.0)
    masks = np.concatenate([first, second, last], 1).astype(np.float32)
    inv = (1.0 / np.float32(10000.0) ** (np.arange(0, HD, 2, dtype=np.float32) / np.float32(HD))).astype(np.float32)
    angle = np.outer(np.arange(LX, dtype=np.float32), inv).astype(np.float32)
    row = np.arange(P) // HH
    cos = np.cos(angle).T[row % (HD // 2)]
    sin = np.sin(angle).T[row % (HD // 2)] * np.where(row < HD // 2, 1.0, -1.0)[:, None]
    return np.eye(P, dtype=np.float32), masks, np.stack([cos, sin]).astype(np.float32)


def kernel(**inputs):
    import concourse.bacc as bacc
    from concourse.bass_utils import run_bass_kernel_spmd

    a = {k: np.asarray(v) for k, v in inputs.items()}
    l0 = {k[len("L0_xattn_"):]: v for k, v in a.items() if k.startswith("L0_xattn_")}
    l1 = {k[len("L1_xattn_"):]: v for k, v in a.items() if k.startswith("L1_xattn_")}
    vec = dict(l0, l1_bq=l1["bq"], l1_bk=l1["bk"], l1_bv=l1["bv"], l1_b1=l1["b1"], l1_b2=l1["b2"],
               ln4_g=l1["ln_g"], ln4_b=l1["ln_b"])
    heads = ("sa_bq", "sa_bk", "ca_bq", "ca_bk", "l1_bq", "l1_bk")
    sq = {"sa_wq": by_head(l0["sa_wq"]), "sa_wk": by_head(l0["sa_wk"]), "sa_wv": l0["sa_wv"], "sa_wo": l0["sa_wo"],
          "ca_wq": by_head(l0["ca_wq"]), "ca_wk": by_head(l0["ca_wk"]), "ca_wv": l0["ca_wv"], "ca_wo": l0["ca_wo"],
          "l1_wq": by_head(l1["Wq"].T), "l1_wk": by_head(l1["Wk"].T), "l1_wv": l1["Wv"].T}
    ident, masks, trig = constants()
    data = {
        "x": a["x"],
        "ctxT": rows_first(np.ascontiguousarray(a["ctx_1024"].transpose(2, 0, 1)).reshape(E, B * LY)),
        **{n: rows_first(w) for n, w in sq.items()},
        "fc1": rows_first(l0["fc1_w"]), "fc2": rows_first(l0["fc2_w"]),
        "l1w1": rows_first(l1["W1"].T), "l1w2": rows_first(l1["W2"].T),
        "cols": np.concatenate([(by_head(vec[n]) if n in heads else vec[n]).reshape(k, P).T
                                for n, (_, k) in COLS.items()], 1),
        "rows": np.concatenate([vec[n] for n in BIAS_ROWS])[None],
        "lnrow": np.broadcast_to(np.stack([l1["ln_g"], l1["ln_b"]])[None], (P, 2, E)),
        "ident": ident, "masks": masks, "trig": trig,
    }
    nc = bacc.Bacc("TRN2", target_bir_lowering=False, num_devices=1, dynamic_dma_scratch_size=1024)
    data = {k: np.ascontiguousarray(v) for k, v in data.items()}
    t = {k: nc.dram_tensor("in_" + k, v.shape, F32, kind="ExternalInput").ap() for k, v in data.items()}
    out = nc.dram_tensor("out", (B, LX, E), F32, kind="ExternalOutput").ap()
    build(nc, t["x"], t["ctxT"], {n: t[n] for n in sq}, (t["fc1"], t["fc2"], t["l1w1"], t["l1w2"]), t["cols"],
          t["rows"], t["lnrow"], t["ident"], t["masks"], t["trig"], out)
    r = run_bass_kernel_spmd(nc, [{"in_" + k: v for k, v in data.items()}], core_ids=[0])
    return r.results[0]["out"]
```

```python
from contextlib import ExitStack

import numpy as np
import concourse.bass as bass
from concourse import mybir

F32 = mybir.dt.float32
BF16 = mybir.dt.bfloat16
I32 = mybir.dt.int32
ALU = mybir.AluOpType
ACT = mybir.ActivationFunctionType
AX = mybir.AxisListType

P = 128
B, LX, LY, E, H, FF = 2, 1024, 154, 256, 16, 1024
HD = E // H
CH = 512
NCHUNK = B * LX // CH
NT = CH // P
HG = 4
NHG = H // HG
KT = E // P
NM = FF // P
HH = H // KT
LYB = LY - P
LYP = 160
NPROD = 6
SROW = NPROD * HD
QPART = (0, 0, 1, 0, 1, 2)
KPART = (0, 1, 0, 2, 1, 0)
NEG = -1.0e30
NORMS = ("ln1", "ln2", "ln3", "ln4")
TWO_ONES = 0x3F803F80
EPS = 1e-5
SCALE = HD ** -0.5
RSQRT_GUESS = 0x5F3759DF

BIAS_ROWS = ("sa_bv", "sa_bo", "ca_bv", "ca_bo", "fc2_b", "l1_bv", "l1_b2")
COLS = {}
for _name, _n in (("ln1_g", KT), ("ln1_b", KT), ("ln2_g", KT), ("ln2_b", KT), ("ln3_g", KT), ("ln3_b", KT),
                  ("ln4_g", KT), ("ln4_b", KT), ("sa_bq", KT), ("sa_bk", KT), ("ca_bq", KT), ("ca_bk", KT),
                  ("l1_bq", KT), ("l1_bk", KT), ("fc1_b", NM), ("l1_b1", NM)):
    COLS[_name] = (sum(n for _, n in COLS.values()), _n)
NCOLS = sum(n for _, n in COLS.values())
NROW = 6
MASKW = 2 * P + P + 2 * P


def units(att, c):
    out = []
    if att == "sa":
        half = c % 2
        for t in range(NT):
            n = (t + 1) * P
            per = {1: 4, 2: 2, 3: 1, 4: 1}[t + 1]
            for h in range(0, HG, per):
                out.append([(t, h + i, half, n, 0, i * n) for i in range(per)])
            if half:
                for h in range(HG):
                    out.append([(t, h, 0, CH, 1, 0)])
    else:
        pairs = [(t, h) for h in range(HG) for t in range(NT)]
        for i in range(0, len(pairs), 3):
            out.append([(t, h, 0, LY, 0, LYP * j) for j, (t, h) in enumerate(pairs[i:i + 3])])
    return out


def groups(att, c):
    return list(range(NT * (c % 2 + 1))) if att == "sa" else ["A", "B"]


def heads(g):
    return range(1 if g == "B" else HG)


def maxes(att, c, hg):
    return [("max", att, c, hg, u) for u in range(len(units(att, c)))] + [("row", att, c, hg)]


def exps(att, c, hg):
    return [("exp", att, c, hg, g, h) for g in groups(att, c) for h in heads(g)]


def weave(main, filler):
    out, done = [], 0
    for i, s in enumerate(main):
        out.append(s)
        while done * len(main) < (i + 1) * len(filler):
            out.append(filler[done])
            done += 1
    return out


def attend(att, c):
    out = maxes(att, c, 0) + maxes(att, c, 1)
    for hg in range(NHG):
        out += weave(exps(att, c, hg), maxes(att, c, hg + 2) if hg + 2 < NHG else [])
    return out


def project(kind, c):
    return [(step, kind, c, f) for f in range(KT) for step in ("proj", "place")]


def cross(att, c):
    return project("q" + att, c) + attend(att, c) + [("drain", att, c)]


def norm(name, c):
    return [("stats", name, c, 0), ("stats", name, c, 1), ("tr", name, c, 0), ("tr", name, c, 1)]


def out_norm(att, name, c):
    return [("tr", "oT_" + att, c, 0), ("tr", "oT_" + att, c, 1), ("wo", att, c, 0), ("stats", name, c, 0),
            ("wo", att, c, 1), ("stats", name, c, 1), ("tr", name, c, 0), ("tr", name, c, 1)]


def mlp(l, c):
    out = [("up", l, c, 0)]
    for m in range(1, NM):
        out += [("up", l, c, m), ("down", l, c, m - 1)]
    return out + [("down", l, c, NM - 1)] + [("res", l, c, g) for g in range(NT // 2)]


def post(c):
    return ([("need", "sa", c)] + out_norm("sa", "ln2", c) + cross("ca", c) + out_norm("ca", "ln3", c)
            + mlp(0, c) + [("tr", "x3", c, g) for g in range(NT // 2)] + cross("la", c)
            + [("addatt", c, g) for g in range(NT // 2)] + norm("ln4", c) + [("lnout", c)] + mlp(1, c)
            + [("store", c)])


def prologue(c):
    out = [("need", "sa", c - 1)] if c and c % 2 == 0 else []
    out += [("load", c)] + norm("ln1", c) + project("ks", c)
    return out + [("v", c, g) for g in range(NT // 2)] + [("done", "pro", c)]


def context():
    return ([("ctxk", l, f) for l in range(2) for f in range(KT)]
            + [("ctxv", l, b) for l in range(2) for b in range(B)] + [("late",)])


def self_attention(c):
    return [("need", "pro", c)] + project("qs", c) + attend("sa", c) + [("drain", "sa", c)]


COST = {"tr": 0.3, "proj": 1.7, "v": 2.0, "wo": 2.0, "up": 1.7, "down": 1.8, "max": 0.25, "row": 0.1,
        "exp": 0.5, "ctxk": 1.1, "ctxv": 2.0}
DELAY = {"stats": 2.5, "tr": 0.8, "place": 4.0, "res": 1.0, "addatt": 1.0, "drain": 3.5, "load": 3.0,
         "ctxk": 2.0}


def order():
    threads = [[s for c in range(NCHUNK) for s in prologue(c)],
               context() + [s for c in range(NCHUNK) for s in post(c)],
               [s for c in range(NCHUNK) for s in self_attention(c)]]
    out, at, ready, now, done = [], [0, 0, 0], [0.0] * 3, 0.0, set()
    item, norming, hidden = None, None, None
    waiting, turning = [], []
    emitted, projected, rowed = set(), [], []

    def due(s):
        if s[0] == "load":
            return s[1] < 2 or ("store", s[1] - 2) in emitted
        if s == ("ctxk", 0, 0) and ("place", "qs", 0, 1) not in emitted:
            return False
        if s[0] in ("proj", "ctxk"):
            return len(projected) < 2 or projected[-2][0] == "ctxk" or ("place", *projected[-2][1:]) in emitted
        if s[0] == "row":
            return len(rowed) < NROW or ("exp", *rowed[-NROW][1:], groups(*rowed[-NROW][1:3])[0], 0) in emitted
        if s[0] == "exp" and s[1] == "sa" and s[2] > 0:
            return ("tr", "oT_sa", s[2] - 1, 1) in emitted
        if s[:2] == ("tr", "ln1") and s[2] > 0:
            return ("proj", "qs", s[2] - 1, KT - 1) in emitted
        return True

    def flush():
        turns = list(turning)
        turning.clear()
        if waiting:
            att, c, hg, g = waiting.pop()
            out.append(("pv", att, c, hg, g))
            if g == groups(att, c)[-1]:
                out.append(("evac", att, c, hg))
                turning.append(("turn", att, c, hg))
        out.extend(turns)

    while any(at[i] < len(threads[i]) for i in range(3)):
        best = None
        for i in range(3):
            if at[i] == len(threads[i]):
                continue
            s = threads[i][at[i]]
            k = s[0]
            if s[0] == "need" and s[1:] not in done:
                continue
            if hidden not in (None, i):
                continue
            if k == "stats" and norming not in (None, i):
                continue
            if k == "up" and norming is not None:
                continue
            if s[0] == "exp" and item not in (None, i):
                continue
            if not due(s):
                continue
            if item == i and s[0] != "exp" and s[0] not in ("max", "row"):
                continue
            if best is None or (ready[i] <= now < ready[best]) or (ready[i] < ready[best] and ready[best] > now):
                best = i
        i, s = best, threads[best][at[best]]
        emitted.add(s)
        if s[0] in ("proj", "ctxk"):
            projected.append(s)
        elif s[0] == "row":
            rowed.append(s)
        at[i] += 1
        k = s[0]
        now = max(now, ready[i]) + COST.get(k, 0)
        ready[i] = now + DELAY.get(k, 0)
        if k == "exp":
            item = i
            out.append(s)
            if s[5] == heads(s[4])[-1]:
                flush()
                waiting.append(s[1:5])
                if s[4] == groups(s[1], s[2])[-1]:
                    item = None
        elif k == "drain":
            flush()
            flush()
            done.add(s[1:])
        elif k == "done":
            done.add(s[1:])
        elif k != "need":
            out.append(s)
        if s[:2] == ("stats", "ln1"):
            norming = i
        elif s[:2] == ("tr", "ln1") and s[3] == 1:
            norming = None
        if k == "up":
            hidden = i
        elif k == "res" and s[3] == NT // 2 - 1:
            hidden = None
    return out


def build(nc, x, ctxT, sq, fcw, cols, rows, lnrow, ident, masks, trig, out):
    ORDER = order()
    nth, seen = {}, {}
    for s in ORDER:
        seen[s[0]] = seen.get(s[0], 0) + 1
        assert s not in nth, s
        nth[s] = seen[s[0]]
    chain_use, misc_use = {}, {}
    for s in ORDER:
        if s[0] in ("ctxk", "ctxv", "tr", "proj", "v", "wo"):
            chain_use[s] = len(chain_use)
        if s[0] == "down" and s[3] == 0:
            for g in range(NT // 2):
                chain_use[("res", s[1], s[2], g)] = len(chain_use)
        if s[0] in ("row", "turn", "up"):
            misc_use[s] = len(misc_use)
    with ExitStack() as ctx:
        def sb(name, shape, dt=F32):
            return ctx.enter_context(nc.sbuf_tensor(name, shape, dt))

        def psum(name):
            return ctx.enter_context(nc.psum_tensor(name, [P, 512], F32))

        def sem(name):
            return ctx.enter_context(nc.semaphore(name))

        w_sq = {n: sb("w_" + n, [P, KT, E]) for n in ("sa_wq", "sa_wk", "sa_wv", "sa_wo", "ca_wq", "ca_wo", "l1_wq")}
        w_up = [sb(f"w_up{l}", [P, KT, FF]) for l in range(2)]
        w_down = [sb(f"w_down{l}", [P, NM, E]) for l in range(2)]
        col = sb("col", [P, NCOLS])
        g4b4 = sb("g4b4", [P, 2, E])
        idf = sb("idf", [P, P])
        idb = sb("idb", [P, P], BF16)
        mask = sb("mask", [P, MASKW], BF16)
        maskw, maskt, maskb = mask[:, 0:2 * P], mask[:, 2 * P:3 * P], mask[:, 3 * P:5 * P]
        cosT = sb("cosT", [P, LX])
        sinT = sb("sinT", [P, LX])
        ones3 = sb("ones3", [3, P], BF16)
        bias3 = sb("bias3", [3, len(BIAS_ROWS), E], BF16)

        KA = sb("KA", [SROW + 2, 2, H, CH], BF16)
        QA = sb("QA", [SROW + 2, H, CH], BF16)
        QC = sb("QC", [SROW + 2, H, CH], BF16)
        KC = sb("KC", [SROW + 2, 2, H, B, LYP], BF16)
        V = sb("V", [P, 2, NT, H, HD + 1])
        VA = sb("VA", [P, 2, B, H, HD + 1])
        VB = sb("VB", [P, 2, B, NHG, HD + 1])
        probs = sb("probs", [P, 2, HG, CH])
        mcol = sb("mcol", [P, NROW, 2, HG, NT])
        mrow = sb("mrow", [HG * NT, NROW, 2, P], BF16)
        osb = sb("osb", [P, CH])
        rec = sb("rec", [P, 2, NT, HG])
        a_sa = sb("a_sa", [P, NT, E])
        a_ctx = sb("a_ctx", [P, NT, E])

        xb = sb("xb", [P, 2, NT, E])
        hT = sb("hT", [P, 2, KT, CH])
        hid = sb("hid", [P, 2, CH])
        rot = sb("rot", [P, 2, CH])
        swap = sb("swap", [P, CH])
        part = sb("part", [P, 2, 3, CH], BF16)
        st6 = sb("st6", [P, NT, 6])
        mv = sb("mv", [P, NT, 2])
        nw = sb("nw", [P, 5, NT])

        xn_pro = hid[:, :, :].rearrange("p a (t e) -> p (a t) e", e=E)

        w_ctx = w_down[1][:, :, :].rearrange("p (n k) e -> p n k e", k=KT)
        cT = a_ctx[:, :, :].rearrange("p a b -> p (a b)")[:, 0:KT * B * LY].rearrange("p (k n) -> p k n", k=KT)
        maskf = rot[:, :, :].rearrange("p a b -> p (a b)")[:, 0:MASKW]
        NB = len(BIAS_ROWS) * E
        brow = w_up[1][0:1, :, :].rearrange("p a b -> p (a b)")[:, 0:NB]
        qflat = QC[0:1, :, :].rearrange("p a b -> p (a b)")
        bpart = [qflat[:, i * NB:(i + 1) * NB] for i in range(3)]

        ps_max = [psum(f"ps_max{i}") for i in range(2)]
        ps_exp = [psum(f"ps_exp{i}") for i in range(2)]
        ps_o = psum("ps_o")
        ps_misc = psum("ps_misc")
        ps_chain = [psum(f"ps_chain{i}") for i in range(2)]

        s_ident_in, s_trig_in, s_cols = sem("ident_in"), sem("trig_in"), sem("cols_in")
        s_mask_in, s_rows_in = sem("mask_in"), sem("rows_in")
        s_wctx, s_wqkv, s_wrest, s_wlate = sem("wctx_in"), sem("wqkv_in"), sem("wrest_in"), sem("wlate_in")
        s_x = [sem(f"x_in{i}") for i in range(2)]
        s_stored = [sem(f"stored{i}") for i in range(2)]
        s_ones = sem("ones_set")
        s_mask = sem("mask_ready")
        s_bpart, s_bmove = sem("bias_parts_ready"), sem("bias_parts_moved")
        s_chain_ready = sem("chain_ready")
        s_chain_free = [sem(f"chain_read{i}") for i in range(2)]
        s_misc_ready, s_misc_free = sem("misc_ready"), sem("misc_read")
        s_max_ready, s_max_done = sem("max_ready"), sem("max_done")
        s_both = sem("two_halves_max")
        s_exp_ready, s_exp_done = sem("exp_ready"), sem("exp_done")
        s_pv, s_evac = sem("pv_done"), sem("o_evacuated")
        s_mput = [sem(f"mrow_placed{i}") for i in range(NROW)]
        s_xn = sem("xn_ready")
        s_part = [sem(f"part{i}_ready") for i in range(3)]
        s_put = {k: [sem(f"placed_{k}{f}") for f in range(KT)] for k in ("qs", "ks", "qc", "kc")}
        s_down = sem("down_done")
        s_scaled = sem("q_weights_scaled")
        s_lnout = sem("ln4_written")
        s_dve, s_pool = sem("dve_chain"), sem("pool_chain")
        block = ctx.enter_context(nc.Block())

        def c0(name, i=0):
            return col[:, COLS[name][0] + i:COLS[name][0] + i + 1]

        def after_chain(eng, s):
            eng.wait_ge(s_chain_free[chain_use[s] % 2], chain_use[s] // 2 + 1)

        def after_misc(eng, s):
            eng.wait_ge(s_misc_free, misc_use[s] + 1)

        def operand(s):
            if s[0] == "ctxk":
                return "kc", s[2]
            return (s[1] if s[1] in ("qs", "ks") else "qc"), s[3]

        proj_nth, put_nth, item_nth, both_nth, exp_nth, put_count = {}, {}, {}, {}, {}, {}
        for s in ORDER:
            if s[0] in ("proj", "ctxk"):
                proj_nth[s] = len(proj_nth) + 1
                put_count[operand(s)] = put_count.get(operand(s), 0) + 1
                put_nth[s] = put_count[operand(s)]
            elif s[0] == "row":
                item_nth[s[1:]] = len(item_nth) + 1
                if s[1] == "sa" and s[2] % 2:
                    both_nth[s[1:]] = len(both_nth) + 1
            elif s[0] == "exp":
                exp_nth[s] = len(exp_nth) + 1
        last_down, downs = {}, 0
        for s in ORDER:
            if s[0] == "down" and s[3] < NM - 1:
                downs += 1
            elif s[0] == "stats":
                last_down[s] = [downs] if downs else []
        last_exp, latest = {}, {}
        for s in ORDER:
            if s[0] == "exp":
                _, att, c, hg, g, h = s
                latest["qs" if att == "sa" else "qc", hg // 2] = exp_nth[s]
                if att == "sa":
                    latest["ks", hg // 2, g // NT] = exp_nth[s]
            elif s[0] == "place":
                _, kind, c, f = s
                key = {"qs": ("qs", f), "ks": ("ks", f, c % 2)}.get(kind, ("qc", f))
                last_exp[s] = latest.get(key)
        projs = sorted(proj_nth, key=proj_nth.get)

        def placed(eng, s):
            key, f = operand(s)
            eng.wait_ge(s_put[key][f], 16 * NPROD * (B if key == "kc" else 1) * put_nth[s])

        @block.sync
        def _(sp):
            def load(c):
                src = x[c // 2, (c % 2) * CH:(c % 2 + 1) * CH, :].rearrange("(t p) e -> p t e", p=P)
                sp.dma_start(xb[:, c % 2, :, :], src).then_inc(s_x[c % 2], 16)

            load(0)
            sp.dma_start(idf[:, :], ident).then_inc(s_ident_in, 16)
            sp.dma_start(col[:, :], cols).then_inc(s_cols, 16)
            for n in ("sa_wk", "sa_wq", "sa_wv"):
                sp.dma_start(w_sq[n][:, :, :], sq[n]).then_inc(s_wqkv, 16)
            sp.dma_start(cosT[:, :], trig[0]).then_inc(s_trig_in, 16)
            sp.dma_start(sinT[:, :], trig[1]).then_inc(s_trig_in, 16)
            sp.dma_start(brow, rows).then_inc(s_rows_in, 16)
            sp.dma_start(maskf, masks).then_inc(s_mask_in, 16)
            sp.dma_start(cT, ctxT).then_inc(s_wctx, 16)
            for i, n in enumerate(("ca_wk", "ca_wv", "l1_wk", "l1_wv")):
                sp.dma_start(w_ctx[:, i], sq[n]).then_inc(s_wctx, 16)
            for n in ("sa_wo", "ca_wq", "ca_wo", "l1_wq"):
                sp.dma_start(w_sq[n][:, :, :], sq[n]).then_inc(s_wrest, 16)
            sp.dma_start(w_up[0][:, :, :], fcw[0]).then_inc(s_wrest, 16)
            sp.dma_start(w_down[0][:, :, :], fcw[1]).then_inc(s_wrest, 16)
            sp.dma_start(g4b4[:, :, :], lnrow).then_inc(s_wrest, 16)
            sp.wait_ge(s_bpart, 3)
            for i in range(3):
                sp.dma_start(bias3[i:i + 1, :, :], bpart[i]).then_inc(s_bmove, 16)
            for s in ORDER:
                k = s[0]
                if k == "load" and s[1] > 0:
                    c = s[1]
                    if c >= 2:
                        sp.wait_ge(s_stored[c % 2], 16 * (c // 2))
                    load(c)
                elif k == "late":
                    after_chain(sp, ("ctxv", 1, B - 1))
                    sp.dma_start(w_up[1][:, :, :], fcw[2]).then_inc(s_wlate, 16)
                    sp.dma_start(w_down[1][:, :, :], fcw[3]).then_inc(s_wlate, 16)
                elif k in ("place", "ctxk"):
                    p = s if k == "ctxk" else ("proj", *s[1:])
                    key, f = operand(p)
                    n = proj_nth[p]
                    which = QPART if key in ("qs", "qc") else KPART
                    if k == "place" and last_exp[s]:
                        sp.wait_ge(s_exp_done, last_exp[s])
                    if key == "qc":
                        sp.wait_ge(s_bmove, 48)
                    for i in range(3):
                        sp.wait_ge(s_part[i], n)
                        for g in range(NPROD):
                            if which[g] != i:
                                continue
                            rows_g = slice(g * HD, (g + 1) * HD)
                            hs = slice(f * HH, (f + 1) * HH)
                            if k == "ctxk":
                                for b in range(B):
                                    sp.dma_start(KC[rows_g, s[1], hs, b, 0:LY],
                                                 part[:, n % 2, i, b * LY:(b + 1) * LY]).then_inc(s_put[key][f], 16)
                            else:
                                dst = {"qs": QA, "ks": KA[:, s[2] % 2], "qc": QC}[key][rows_g, hs, :]
                                sp.dma_start(dst, part[:, n % 2, i, :]).then_inc(s_put[key][f], 16)
                elif k == "row":
                    _, att, c, hg = s
                    n = item_nth[s[1:]]
                    after_misc(sp, s)
                    q, h0 = QA if att == "sa" else QC, hg * HG
                    for i in range(2):
                        sp.dma_start(q[SROW + i:SROW + i + 1, h0:h0 + HG, :],
                                     mrow[:, n % NROW, i, :]).then_inc(s_mput[n % NROW], 16)
                elif k == "store":
                    c = s[1]
                    for g in range(NT // 2):
                        after_chain(sp, ("res", 1, c, g))
                    dst = out[c // 2, (c % 2) * CH:(c % 2 + 1) * CH, :].rearrange("(t p) e -> p t e", p=P)
                    sp.dma_start(dst, xb[:, c % 2, :, :]).then_inc(s_stored[c % 2], 16)
            for i in range(2):
                sp.wait_ge(s_stored[i], 16 * (NCHUNK // 2))

        @block.tensor
        def _(pe):
            pe.wait_ge(s_ident_in, 16)
            n_max = [0]

            def chain_bank(s):
                n = chain_use[s]
                if n >= 2:
                    pe.wait_ge(s_chain_free[n % 2], n // 2)
                return ps_chain[n % 2]

            def misc_bank(s):
                n = misc_use[s]
                if n >= 1:
                    pe.wait_ge(s_misc_free, n)
                return ps_misc

            waited = set()

            def once(key, s, v):
                if key not in waited:
                    waited.add(key)
                    pe.wait_ge(s, v)

            def add_bias(dst, name, m=P, start=True):
                once("bias", s_bmove, 48)
                once("mask", s_mask, 3)
                i = BIAS_ROWS.index(name)
                pe.matmul(dst, ones3[0:3, 0:m], bias3[0:3, i, :], start=start, stop=False, skip_group_check=True)

            for s in ORDER:
                k = s[0]
                if k == "ctxk":
                    _, l, f = s
                    once("wctx", s_wctx, 80)
                    bank = chain_bank(s)
                    for t in range(KT):
                        mm = pe.matmul(bank[:, 0:B * LY], w_ctx[:, 2 * l, t, f * P:(f + 1) * P], cT[:, t, :],
                                       start=(t == 0), stop=(t == KT - 1))
                    mm.then_inc(s_chain_ready, 1)
                elif k == "ctxv":
                    _, l, b = s
                    bank = chain_bank(s)
                    name = ("ca_bv", "l1_bv")[l]
                    add_bias(bank[:, 0:E], name)
                    for t in range(KT):
                        pe.matmul(bank[:, 0:E], cT[:, t, b * LY:b * LY + P], w_ctx[:, 2 * l + 1, t, :],
                                  start=False, stop=(t == KT - 1), skip_group_check=True)
                    for j in range(HG):
                        dst = bank[32 * j:32 * j + LYB, E:2 * E]
                        add_bias(dst, name, LYB, start=False)
                        for t in range(KT):
                            mm = pe.matmul(dst, cT[:, t, b * LY + P:(b + 1) * LY], w_ctx[:, 2 * l + 1, t, :],
                                           start=False, stop=(t == KT - 1), skip_group_check=True)
                    mm.then_inc(s_chain_ready, 1)
                elif k == "tr":
                    _, what, c, g = s
                    if what in NORMS:
                        pe.wait_ge(s_xn, nth[("stats", what, c, g)])
                        src = xn_pro if what == "ln1" else a_ctx
                    elif what == "x3":
                        after_chain(pe, ("res", 0, c, g))
                        src = xb[:, c % 2]
                    else:
                        att = what[3:]
                        after_misc(pe, ("turn", att, c, NHG - 1))
                        src = a_sa if att == "sa" else a_ctx
                    bank = chain_bank(s)
                    for f in range(KT):
                        for t in range(2):
                            mm = pe.transpose(bank[:, (2 * f + t) * P:(2 * f + t + 1) * P],
                                              src[:, 2 * g + t, f * P:(f + 1) * P], idf[:, :])
                    mm.then_inc(s_chain_ready, 1)
                elif k in ("proj", "v", "wo"):
                    what = "ln1" if k == "v" or (k == "proj" and s[1] in ("qs", "ks")) else None
                    if k == "v":
                        name, c = "sa_wv", s[1]
                    elif k == "wo":
                        name, c = s[1] + "_wo", s[2]
                        what = "oT_" + s[1]
                    else:
                        name, c = {"qs": "sa_wq", "ks": "sa_wk", "qca": "ca_wq", "qla": "l1_wq"}[s[1]], s[2]
                        what = what or {"qca": "ln2", "qla": "x3"}[s[1]]
                    once("wqkv", s_wqkv, 48)
                    if what != "ln1":
                        once("wrest", s_wrest, 16 * 7)
                    for g in range(NT // 2):
                        if k == "proj" or g == s[-1]:
                            after_chain(pe, ("tr", what, c, g))
                    src = hT[:, 0 if what == "ln1" else 1]
                    w = w_sq[name]
                    if name.endswith("_wq"):
                        once(name, s_scaled, {"sa_wq": 4, "ca_wq": 5, "l1_wq": 6}[name])
                    bank = chain_bank(s)
                    if k == "proj":
                        f = s[3]
                        for t in range(KT):
                            mm = pe.matmul(bank[:, :], w[:, t, f * P:(f + 1) * P], src[:, t, :],
                                           start=(t == 0), stop=(t == KT - 1))
                    else:
                        for i in range(2):
                            dst = bank[:, i * E:(i + 1) * E]
                            add_bias(dst, "sa_bv" if k == "v" else s[1] + "_bo")
                            tok = (2 * s[-1] + i) * P
                            for t in range(KT):
                                mm = pe.matmul(dst, src[:, t, tok:tok + P], w[:, t, :],
                                               start=False, stop=(t == KT - 1), skip_group_check=True)
                    mm.then_inc(s_chain_ready, 1)
                elif k == "up":
                    _, l, c, m = s
                    for g in range(NT // 2):
                        after_chain(pe, ("tr", ("ln3", "ln4")[l], c, g))
                    if l:
                        once("wlate", s_wlate, 32)
                    elif m == 0:
                        once("wrest", s_wrest, 16 * 7)
                    bank = misc_bank(s)
                    for t in range(KT):
                        mm = pe.matmul(bank[:, :], w_up[l][:, t, m * P:(m + 1) * P], hT[:, 1, t, :],
                                       start=(t == 0), stop=(t == KT - 1))
                    mm.then_inc(s_misc_ready, 1)
                elif k == "down":
                    _, l, c, m = s
                    banks = []
                    for g in range(NT // 2):
                        use = ("res", l, c, g)
                        banks.append(chain_bank(use) if m == 0 else ps_chain[chain_use[use] % 2])
                    after_misc(pe, ("up", l, c, m))
                    for t in range(NT):
                        dst = banks[t // 2][:, (t % 2) * E:(t % 2 + 1) * E]
                        if m == 0:
                            add_bias(dst, ("fc2_b", "l1_b2")[l], start=(t % 2 == 0))
                        mm = pe.matmul(dst, hid[:, m % 2, t * P:(t + 1) * P], w_down[l][:, m, :],
                                       start=False, stop=(m == NM - 1), skip_group_check=True)
                        if m == NM - 1 and t % 2:
                            mm.then_inc(s_chain_ready, 1)
                        elif t == NT - 1:
                            mm.then_inc(s_down, 1)
                elif k == "max":
                    _, att, c, hg, u = s
                    unit = units(att, c)[u]
                    once("mask", s_mask, 3)
                    once("ones", s_ones, 1)
                    if u == 0:
                        f = hg // 2
                        if att == "sa":
                            placed(pe, ("proj", "qs", c, f))
                            placed(pe, ("proj", "ks", c, f))
                        else:
                            placed(pe, ("proj", "q" + att, c, f))
                            once(("kc", f), s_put["kc"][f], 16 * NPROD * B * 2)
                    if n_max[0] >= 2:
                        pe.wait_ge(s_max_done, n_max[0] - 1)
                    bank = ps_max[n_max[0] % 2]
                    n_max[0] += 1
                    for t, h, half, n, pt, at0 in unit:
                        dst = bank[:, at0:at0 + n]
                        if att == "sa":
                            q = QA[0:SROW, hg * HG + h, t * P:(t + 1) * P]
                            kk = KA[0:SROW, half, hg * HG + h, 0:n]
                            causal = [(n - P, P, maskw[:, 0:P])] if pt == 0 else []
                        else:
                            l = int(att == "la")
                            q = QC[0:SROW, hg * HG + h, t * P:(t + 1) * P]
                            kk = KC[0:SROW, l, hg * HG + h, c // 2, 0:LY]
                            causal = []
                            if l and c % 2 == 0 and t < 2:
                                causal = [[(0, LY, maskw[:, 0:LY])], [(P, LYB, maskw[:, 0:LYB])]][t]
                        mm = pe.matmul(dst, q, kk, start=True, stop=not causal)
                        for a0, w0, mk in causal:
                            mm = pe.matmul(bank[:, at0 + a0:at0 + a0 + w0], idb[:, :], mk, start=False, stop=True)
                    mm.then_inc(s_max_ready, 1)
                elif k == "row":
                    n = item_nth[s[1:]]
                    _, att, c, hg = s
                    if s[1:] in both_nth:
                        pe.wait_ge(s_both, both_nth[s[1:]])
                    else:
                        pe.wait_ge(s_max_done, nth[("max", att, c, hg, len(units(att, c)) - 1)])
                    bank = misc_bank(s)
                    src = mcol[:, n % NROW, 0, :, :].rearrange("p h t -> p (h t)")
                    pe.transpose(bank[0:NT * HG, 0:P], src, idf[:, :]).then_inc(s_misc_ready, 1)
                elif k == "exp":
                    _, att, c, hg, g, h = s
                    if g == groups(att, c)[0] and h == 0:
                        n = item_nth[(att, c, hg)]
                        pe.wait_ge(s_mput[n % NROW], 32 * ((n - 1) // NROW + 1))
                    n = exp_nth[s]
                    if n > 2:
                        pe.wait_ge(s_exp_done, n - 2)
                    bank = ps_exp[n % 2]
                    l = int(att == "la")
                    hh = hg * HG + h
                    causal = l and c % 2 == 0
                    if att == "sa":
                        r = g - NT * (c % 2)
                        q0 = max(r, 0) * P
                        mm = pe.matmul(bank[:, q0:CH], KA[:, g // NT, hh, (g % NT) * P:(g % NT + 1) * P],
                                       QA[:, hh, q0:CH], start=True, stop=(r < 0))
                        if r >= 0:
                            mm = pe.matmul(bank[:, q0:q0 + P], idb[:, :], maskt, start=False, stop=True)
                    elif g == "A":
                        mm = pe.matmul(bank[:, :], KC[:, l, hh, c // 2, 0:P], QC[:, hg * HG + h, :],
                                       start=True, stop=not causal)
                        if causal:
                            mm = pe.matmul(bank[:, 0:P], idb[:, :], maskt, start=False, stop=True)
                    else:
                        for h in range(HG):
                            mm = pe.matmul(bank[32 * h:32 * h + 32, :], KC[:, l, hg * HG + h, c // 2, P:LYP],
                                           QC[:, hg * HG + h, :], start=True, stop=not causal,
                                           skip_group_check=True)
                        if causal:
                            mm = pe.matmul(bank[:, 0:2 * P], idb[:, :], maskb, start=False, stop=True,
                                           skip_group_check=True)
                    mm.then_inc(s_exp_ready, 1)
                elif k == "pv":
                    _, att, c, hg, g = s
                    n = nth[s]
                    pe.wait_ge(s_exp_done, exp_nth[("exp", att, c, hg, g, heads(g)[-1])])
                    first = g == groups(att, c)[0]
                    last = g == groups(att, c)[-1]
                    if first:
                        item = nth[("evac", att, c, hg)]
                        if item > 1:
                            pe.wait_ge(s_evac, item - 1)
                        if att == "sa":
                            for i in range(NT // 2):
                                after_chain(pe, ("v", c, i))
                    for h in range(HG):
                        hh = hg * HG + h
                        p0, q0 = 32 * h, 0
                        if att == "sa":
                            q0 = max(g - NT * (c % 2), 0) * P
                            v, pr = V[:, g // NT, g % NT, hh, :], probs[:, n % 2, h, q0:CH]
                        elif g == "A":
                            v, pr = VA[:, int(att == "la"), c // 2, hh, :], probs[:, n % 2, h, :]
                        else:
                            v = VB[p0:p0 + LYB, int(att == "la"), c // 2, hg, :]
                            pr = probs[p0:p0 + LYB, n % 2, 0, :]
                        mm = pe.matmul(ps_o[p0:p0 + HD + 1, q0:CH], v, pr, start=first, stop=last,
                                       skip_group_check=True)
                    mm.then_inc(s_pv, 1)
                elif k == "turn":
                    n = nth[s]
                    pe.wait_ge(s_evac, n)
                    bank = misc_bank(s)
                    for t in range(NT):
                        mm = pe.transpose(bank[:, t * P:(t + 1) * P], osb[:, t * P:(t + 1) * P], idf[:, :])
                    mm.then_inc(s_misc_ready, 1)

        @block.vector
        def _(dve):
            chain = [0]

            def link(ins):
                chain[0] += 1
                ins.then_inc(s_dve, 1)
                dve.wait_ge(s_dve, chain[0])

            dve.wait_ge(s_scaled, 3)
            for s in ORDER:
                k = s[0]
                if s == ("tr", "ln1", 0, 0):
                    dve.memset(ps_o[:, :], 0.0)
                    dve.wait_ge(s_mask_in, 16)
                    dve.tensor_copy(mask[:, :], maskf).then_inc(s_mask, 1)
                    dve.tensor_copy(idb[:, :], idf[:, :]).then_inc(s_mask, 1)
                    dve.memset(ones3[:, :], 1.0).then_inc(s_mask, 1)
                if s == ("place", "ks", 0, 0):
                    dve.wait_ge(s_rows_in, 16)
                    for i in range(3):
                        dve.tensor_copy(bpart[i], brow).then_inc(s_bpart, 1)
                        if i < 2:
                            dve.wait_ge(s_bpart, i + 1)
                            link(dve.tensor_tensor(brow, brow, bpart[i], ALU.subtract))
                if k in ("ctxk", "proj"):
                    n = proj_nth[s]
                    u = chain_use[s]
                    i = n % 2
                    bank = ps_chain[u % 2]
                    if k == "ctxk":
                        rope, name, f = s[1] == 0, ("ca_bk", "l1_bk")[s[1]], s[2]
                        pieces = [(b * LY, 0, LY) for b in range(B)]
                        width = B * LY
                    else:
                        kind, c, f = s[1:]
                        rope, name = kind != "qla", {"qs": "sa_bq", "ks": "sa_bk", "qca": "ca_bq", "qla": "l1_bq"}[kind]
                        pieces = [(0, (c % 2) * CH, CH)]
                        width = CH
                    if n > 2:
                        placed(dve, projs[n - 3])
                        dve.wait_ge(s_part[2], n - 2)
                    elif n == 1:
                        dve.wait_ge(s_mask, 2)
                    dve.wait_ge(s_chain_ready, u + 1)
                    r, w = rot[:, i, 0:width], swap[:, 0:width]
                    p1, p2 = part[:, i, 0, 0:width], part[:, i, 1, 0:width]
                    bc = c0(name, f)
                    if rope:
                        if n == 1:
                            dve.wait_ge(s_trig_in, 32)
                        for a0, t0, wd in pieces:
                            for lo, hi in ((0, 64), (64, 0)):
                                dve.scalar_tensor_tensor(w[lo:lo + 64, a0:a0 + wd], bank[hi:hi + 64, a0:a0 + wd],
                                                         bc[hi:hi + 64], sinT[hi:hi + 64, t0:t0 + wd], ALU.add, ALU.mult)
                            ins = dve.scalar_tensor_tensor(r[:, a0:a0 + wd], bank[:, a0:a0 + wd], bc,
                                                           cosT[:, t0:t0 + wd], ALU.add, ALU.mult)
                        ins.then_inc(s_chain_free[u % 2], 1)
                        after_chain(dve, s)
                        link(dve.tensor_tensor(r, r, w, ALU.add))
                    else:
                        dve.tensor_scalar(r, bank[:, 0:width], bc, None, ALU.add).then_inc(s_chain_free[u % 2], 1)
                        after_chain(dve, s)
                    dve.tensor_copy(p1, r).then_inc(s_part[0], 1)
                    dve.wait_ge(s_part[0], n)
                    link(dve.tensor_tensor(r, r, p1, ALU.subtract))
                    dve.tensor_copy(p2, r).then_inc(s_part[1], 1)
                elif k == "wo" or k == "res":
                    c = s[2]
                    u = chain_use[s]
                    g = s[3]
                    dve.wait_ge(s_chain_ready, u + 1)
                    if k == "res" and s[1] == 1:
                        dve.wait_ge(s_lnout, c + 1)
                    xs = xb[:, c % 2, 2 * g:2 * g + 2, :].rearrange("p t e -> p (t e)")
                    dve.tensor_tensor(xs, xs, ps_chain[u % 2][:, :], ALU.add).then_inc(s_chain_free[u % 2], 1)
                elif k == "addatt":
                    _, c, g = s
                    after_misc(dve, ("turn", "la", c, NHG - 1))
                    xs = xb[:, c % 2, 2 * g:2 * g + 2, :]
                    link(dve.tensor_tensor(xs, xs, a_ctx[:, 2 * g:2 * g + 2, :], ALU.add))
                elif k == "stats":
                    _, what, c, g = s
                    tiles = (2 * g, 2 * g + 1)
                    if what == "ln1":
                        dve.wait_ge(s_x[c % 2], 16 * (c // 2 + 1))
                    elif what != "ln4":
                        after_chain(dve, ("wo", {"ln2": "sa", "ln3": "ca"}[what], c, g))
                    for t in tiles:
                        ins = dve.bn_stats(st6[:, t, :], xb[:, c % 2, t, :])
                    link(ins)
                    for t in tiles:
                        ins = dve.bn_aggr(mv[:, t, :], st6[:, t, :])
                    link(ins)
                    v, y, t1, t2 = (nw[:, i, 2 * g:2 * g + 2] for i in range(4))
                    link(dve.tensor_scalar(v, mv[:, 2 * g:2 * g + 2, 1], EPS, None, ALU.add))
                    link(dve.tensor_scalar(t1.bitcast(I32), v.bitcast(I32), 1, None, ALU.logical_shift_right))
                    link(dve.tensor_scalar(y.bitcast(I32), t1.bitcast(I32), -1, RSQRT_GUESS, ALU.mult, ALU.add))
                    for _ in range(3):
                        link(dve.tensor_tensor(t1, y, y, ALU.mult))
                        link(dve.scalar_tensor_tensor(t2, t1, -0.5, v, ALU.mult, ALU.mult))
                        link(dve.scalar_tensor_tensor(y, t2, 1.5, y, ALU.add, ALU.mult))
                    if g == 0:
                        if what == "ln1" and c > 0:
                            dve.wait_ge(s_chain_ready, chain_use[("tr", "ln1", c - 1, 1)] + 1)
                            for m in last_down[s]:
                                dve.wait_ge(s_down, m)
                        elif what in ("ln2", "ln3"):
                            dve.wait_ge(s_chain_ready, chain_use[("tr", {"ln2": "oT_sa", "ln3": "oT_ca"}[what], c, 1)] + 1)
                            if what == "ln2" and c > 0:
                                dve.wait_ge(s_lnout, c)
                            if what == "ln2" and c == 0:
                                dve.wait_ge(s_chain_ready, chain_use[("ctxv", 1, B - 1)] + 1)
                    dst = xn_pro if what == "ln1" else a_ctx
                    for i, t in enumerate(tiles):
                        ins = dve.tensor_scalar(dst[:, t, :], xb[:, c % 2, t, :], mv[:, t, 0:1], y[:, i:i + 1],
                                                ALU.subtract, ALU.mult)
                    ins.then_inc(s_xn, 1)
                elif k == "max":
                    _, att, c, hg, u = s
                    unit = units(att, c)[u]
                    n = item_nth[(att, c, hg)]
                    dve.wait_ge(s_max_ready, nth[s])
                    bank = ps_max[(nth[s] - 1) % 2]
                    t, h, _, w, pt, _ = unit[0]
                    step = w if att == "sa" else LYP
                    src = bank[:, 0:len(unit) * step].rearrange("p (n w) -> p n w", w=step)[:, :, 0:w]
                    if att == "sa":
                        dst = mcol[:, n % NROW, pt, h:h + len(unit), t]
                    else:
                        k0 = h * NT + t
                        dst = mcol[:, n % NROW, 0, :, :].rearrange("p h t -> p (h t)")[:, k0:k0 + len(unit)]
                    dve.tensor_reduce(dst, src, AX.X, ALU.max).then_inc(s_max_done, 1)
                elif k == "row":
                    _, att, c, hg = s
                    n = item_nth[s[1:]]
                    if s[1:] in both_nth:
                        dve.wait_ge(s_max_done, nth[("max", att, c, hg, len(units(att, c)) - 1)])
                        m0, m1 = mcol[:, n % NROW, 0, :, :], mcol[:, n % NROW, 1, :, :]
                        dve.tensor_tensor(m0, m0, m1, ALU.max).then_inc(s_both, 1)
                    dve.wait_ge(s_misc_ready, misc_use[s] + 1)
                    src = ps_misc[0:NT * HG, 0:P]
                    link(dve.tensor_scalar(mrow[:, n % NROW, 0, :], src, -1.0, None, ALU.mult))
                    dve.scalar_tensor_tensor(mrow[:, n % NROW, 1, :], src, -1.0, mrow[:, n % NROW, 0, :],
                                             ALU.mult, ALU.subtract).then_inc(s_misc_free, 1)
                elif k == "turn":
                    _, att, c, hg = s
                    n = nth[s]
                    dve.wait_ge(s_misc_ready, misc_use[s] + 1)
                    src = ps_misc[:, :].rearrange("p (t h w) -> p t h w", t=NT, h=HG)
                    r = rec[:, n % 2]
                    link(dve.reciprocal(r, src[:, :, :, HD]))
                    dst = (a_sa if att == "sa" else a_ctx)[:, :, hg * HG * HD:(hg + 1) * HG * HD]
                    dst = dst.rearrange("p t (h d) -> p t h d", h=HG)
                    rb = r.unsqueeze(3).to_broadcast([P, NT, HG, HD])
                    dve.tensor_tensor(dst, src[:, :, :, 0:HD], rb, ALU.mult).then_inc(s_misc_free, 1)

        @block.scalar
        def _(act):
            act.wait_ge(s_cols, 16)
            turns = [s for s in ORDER if s[0] == "turn"]
            for s in ORDER:
                k = s[0]
                if k in ("tr", "v", "ctxv"):
                    u = chain_use[s]
                    act.wait_ge(s_chain_ready, u + 1)
                    bank = ps_chain[u % 2]
                if k == "tr":
                    _, what, c, g = s
                    dst = hT[:, 0 if what == "ln1" else 1, :, 2 * g * P:(2 * g + 2) * P]
                    src = bank[:, :].rearrange("p (f n) -> p f n", f=KT)
                    if what in NORMS:
                        for f in range(KT):
                            ins = act.activation(dst[:, f, :], src[:, f, :], ACT.Identity,
                                                 bias=c0(what + "_b", f), scale=c0(what + "_g", f))
                    else:
                        ins = act.activation(dst, src, ACT.Copy)
                    ins.then_inc(s_chain_free[u % 2], 1)
                elif k == "v":
                    _, c, g = s
                    act.activation(V[:, c % 2, 2 * g:2 * g + 2, :, 0:HD],
                                   bank[:, :].rearrange("p (t h d) -> p t h d", t=2, h=H),
                                   ACT.Copy).then_inc(s_chain_free[u % 2], 1)
                elif k == "ctxv":
                    _, l, b = s
                    act.activation(VA[:, l, b, :, 0:HD], bank[:, 0:E].rearrange("p (h d) -> p h d", h=H), ACT.Copy)
                    for j in range(HG):
                        q = slice(32 * j, 32 * j + LYB)
                        src = bank[q, E:2 * E].rearrange("p (g h d) -> p g h d", g=NHG, h=HG)[:, :, j, :]
                        ins = act.activation(VB[q, l, b, :, 0:HD], src, ACT.Copy)
                    ins.then_inc(s_chain_free[u % 2], 1)
                elif k == "up":
                    _, l, c, m = s
                    act.wait_ge(s_misc_ready, misc_use[s] + 1)
                    act.activation(hid[:, m % 2, :], ps_misc[:, :], (ACT.Gelu_apprx_tanh, ACT.Gelu)[l],
                                   bias=c0(("fc1_b", "l1_b1")[l], m)).then_inc(s_misc_free, 1)
                elif k == "exp":
                    _, att, c, hg, g, h = s
                    n = nth[("pv", att, c, hg, g)]
                    if n > 2 and h == 0:
                        act.wait_ge(s_pv, n - 2)
                    act.wait_ge(s_exp_ready, exp_nth[s])
                    q0 = max(g - NT * (c % 2), 0) * P if att == "sa" else 0
                    act.activation(probs[:, n % 2, h, q0:CH], ps_exp[exp_nth[s] % 2][:, q0:CH],
                                   ACT.Exp).then_inc(s_exp_done, 1)
                elif k == "evac":
                    _, att, c, hg = s
                    act.wait_ge(s_pv, nth[("pv", att, c, hg, groups(att, c)[-1])])
                    if nth[s] > 1:
                        act.wait_ge(s_misc_ready, misc_use[turns[nth[s] - 2]] + 1)
                    act.activation(osb[:, :], ps_o[:, :], ACT.Copy).then_inc(s_evac, 1)

        @block.gpsimd
        def _(pool):
            chain = [0]

            def link(ins):
                chain[0] += 1
                ins.then_inc(s_pool, 1)
                pool.wait_ge(s_pool, chain[0])

            def scale(a, n):
                pool.tensor_scalar(a, a, SCALE, None, ALU.mult).then_inc(s_scaled, 1)
                pool.wait_ge(s_scaled, n)

            pool.wait_ge(s_cols, 16)
            for i, name in enumerate(("sa_bq", "ca_bq", "l1_bq")):
                scale(col[:, COLS[name][0]:COLS[name][0] + KT], i + 1)
            link(pool.memset(KA[SROW:SROW + 2, 0, :, :].bitcast(I32), TWO_ONES))
            link(pool.memset(V[:, :, :, :, HD:HD + 1], 1.0))
            pool.wait_ge(s_wqkv, 48)
            scale(w_sq["sa_wq"][:, :, :], 4)
            for s in ORDER:
                k = s[0]
                if s == ("v", 0, 0):
                    pool.wait_ge(s_part[2], n)
                    link(pool.memset(KA[SROW:SROW + 2, 1, :, :].bitcast(I32), TWO_ONES))
                    link(pool.memset(KC[0:SROW, :, :, :, LY:LYP], 0.0))
                    link(pool.memset(KC[SROW:SROW + 2, :, :, :, :].bitcast(I32), TWO_ONES))
                    link(pool.memset(VA[:, :, :, :, HD:HD + 1], 1.0))
                    pool.memset(VB[:, :, :, :, HD:HD + 1], 1.0).then_inc(s_ones, 1)
                    pool.wait_ge(s_ones, 1)
                    pool.wait_ge(s_wrest, 16 * 7)
                    scale(w_sq["ca_wq"][:, :, :], 5)
                    scale(w_sq["l1_wq"][:, :, :], 6)
                if k in ("proj", "ctxk"):
                    n = proj_nth[s]
                    width = B * LY if k == "ctxk" else CH
                    pool.wait_ge(s_part[1], n)
                    pool.tensor_tensor(part[:, n % 2, 2, 0:width], rot[:, n % 2, 0:width],
                                       part[:, n % 2, 1, 0:width], ALU.subtract).then_inc(s_part[2], 1)
                elif k == "lnout":
                    c = s[1]
                    pool.wait_ge(s_xn, nth[("stats", "ln4", c, 1)])
                    for i, op in enumerate((ALU.mult, ALU.add)):
                        for t in range(NT):
                            ins = pool.tensor_tensor(xb[:, c % 2, t, :], (a_ctx if i == 0 else xb[:, c % 2])[:, t, :],
                                                     g4b4[:, i, :], op)
                        if i == 0:
                            link(ins)
                    ins.then_inc(s_lnout, 1)


def rows_first(a):
    return np.ascontiguousarray(a.reshape(-1, P, a.shape[1]).transpose(1, 0, 2))


def by_head(a):
    return a.reshape(a.shape[:-1] + (KT, HH, HD)).swapaxes(-1, -2).reshape(a.shape)


def constants():
    q, k = np.arange(P)[:, None], np.arange(2 * P)[None, :]
    first = np.where(k > q, NEG, 0.0)
    second = np.where(q > k[:, :P], NEG, 0.0)
    last = np.where(P + q % 32 > k, NEG, 0.0)
    masks = np.concatenate([first, second, last], 1).astype(np.float32)
    inv = (1.0 / np.float32(10000.0) ** (np.arange(0, HD, 2, dtype=np.float32) / np.float32(HD))).astype(np.float32)
    angle = np.outer(np.arange(LX, dtype=np.float32), inv).astype(np.float32)
    row = np.arange(P) // HH
    cos = np.cos(angle).T[row % (HD // 2)]
    sin = np.sin(angle).T[row % (HD // 2)] * np.where(row < HD // 2, 1.0, -1.0)[:, None]
    return np.eye(P, dtype=np.float32), masks, np.stack([cos, sin]).astype(np.float32)


def kernel(**inputs):
    import concourse.bacc as bacc
    from concourse.bass_utils import run_bass_kernel_spmd

    a = {k: np.asarray(v) for k, v in inputs.items()}
    l0 = {k[len("L0_xattn_"):]: v for k, v in a.items() if k.startswith("L0_xattn_")}
    l1 = {k[len("L1_xattn_"):]: v for k, v in a.items() if k.startswith("L1_xattn_")}
    vec = dict(l0, l1_bq=l1["bq"], l1_bk=l1["bk"], l1_bv=l1["bv"], l1_b1=l1["b1"], l1_b2=l1["b2"],
               ln4_g=l1["ln_g"], ln4_b=l1["ln_b"])
    heads = ("sa_bq", "sa_bk", "ca_bq", "ca_bk", "l1_bq", "l1_bk")
    sq = {"sa_wq": by_head(l0["sa_wq"]), "sa_wk": by_head(l0["sa_wk"]), "sa_wv": l0["sa_wv"], "sa_wo": l0["sa_wo"],
          "ca_wq": by_head(l0["ca_wq"]), "ca_wk": by_head(l0["ca_wk"]), "ca_wv": l0["ca_wv"], "ca_wo": l0["ca_wo"],
          "l1_wq": by_head(l1["Wq"].T), "l1_wk": by_head(l1["Wk"].T), "l1_wv": l1["Wv"].T}
    ident, masks, trig = constants()
    data = {
        "x": a["x"],
        "ctxT": rows_first(np.ascontiguousarray(a["ctx_1024"].transpose(2, 0, 1)).reshape(E, B * LY)),
        **{n: rows_first(w) for n, w in sq.items()},
        "fc1": rows_first(l0["fc1_w"]), "fc2": rows_first(l0["fc2_w"]),
        "l1w1": rows_first(l1["W1"].T), "l1w2": rows_first(l1["W2"].T),
        "cols": np.concatenate([(by_head(vec[n]) if n in heads else vec[n]).reshape(k, P).T
                                for n, (_, k) in COLS.items()], 1),
        "rows": np.concatenate([vec[n] for n in BIAS_ROWS])[None],
        "lnrow": np.broadcast_to(np.stack([l1["ln_g"], l1["ln_b"]])[None], (P, 2, E)),
        "ident": ident, "masks": masks, "trig": trig,
    }
    nc = bacc.Bacc("TRN2", target_bir_lowering=False, num_devices=1, dynamic_dma_scratch_size=1024)
    data = {k: np.ascontiguousarray(v) for k, v in data.items()}
    t = {k: nc.dram_tensor("in_" + k, v.shape, F32, kind="ExternalInput").ap() for k, v in data.items()}
    out = nc.dram_tensor("out", (B, LX, E), F32, kind="ExternalOutput").ap()
    build(nc, t["x"], t["ctxT"], {n: t[n] for n in sq}, (t["fc1"], t["fc2"], t["l1w1"], t["l1w2"]), t["cols"],
          t["rows"], t["lnrow"], t["ident"], t["masks"], t["trig"], out)
    r = run_bass_kernel_spmd(nc, [{"in_" + k: v for k, v in data.items()}], core_ids=[0])
    return r.results[0]["out"]
```

```python
from contextlib import ExitStack

import numpy as np
import concourse.bass as bass
from concourse import mybir

F32 = mybir.dt.float32
BF16 = mybir.dt.bfloat16
I32 = mybir.dt.int32
ALU = mybir.AluOpType
ACT = mybir.ActivationFunctionType
AX = mybir.AxisListType

P = 128
B, LX, LY, E, H, FF = 2, 1024, 154, 256, 16, 1024
HD = E // H
CH = 512
NCHUNK = B * LX // CH
LAST = NCHUNK - 1
NT = CH // P
HG = 4
NHG = H // HG
KT = E // P
NM = FF // P
HH = H // KT
LYB = LY - P
LYP = 160
NPROD = 6
SROW = NPROD * HD
QPART = (0, 0, 1, 0, 1, 2)
KPART = (0, 1, 0, 2, 1, 0)
NEG = -1.0e30
NORMS = ("ln1", "ln2", "ln3", "ln4")
TWO_ONES = 0x3F803F80
EPS = 1e-5
SCALE = HD ** -0.5
RSQRT_GUESS = 0x5F3759DF

BIAS_ROWS = ("sa_bv", "sa_bo", "ca_bv", "ca_bo", "fc2_b", "l1_bv", "l1_b2")
COLS = {}
for _name, _n in (("ln1_g", KT), ("ln1_b", KT), ("ln2_g", KT), ("ln2_b", KT), ("ln3_g", KT), ("ln3_b", KT),
                  ("ln4_g", KT), ("ln4_b", KT), ("sa_bq", KT), ("sa_bk", KT), ("ca_bq", KT), ("ca_bk", KT),
                  ("l1_bq", KT), ("l1_bk", KT), ("fc1_b", NM), ("l1_b1", NM)):
    COLS[_name] = (sum(n for _, n in COLS.values()), _n)
NCOLS = sum(n for _, n in COLS.values())
NROW = {"q": 4, "c": 3}
MASKW = 2 * P + P + 2 * P


def units(att, c):
    out = []
    if att == "sa":
        half = c % 2
        for t in range(NT):
            n = (t + 1) * P
            per = {1: 4, 2: 2, 3: 1, 4: 1}[t + 1]
            for h in range(0, HG, per):
                out.append([(t, h + i, half, n, 0, i * n) for i in range(per)])
            if half:
                for h in range(HG):
                    out.append([(t, h, 0, CH, 1, 0)])
    else:
        pairs = [(t, h) for h in range(HG) for t in range(NT)]
        for i in range(0, len(pairs), 3):
            out.append([(t, h, 0, LY, 0, LYP * j) for j, (t, h) in enumerate(pairs[i:i + 3])])
    return out


def groups(att, c):
    return list(range(NT * (c % 2 + 1))) if att == "sa" else ["A", "B"]


def heads(g):
    return range(1 if g == "B" else HG)


def side(att, c):
    return "q" if att == "sa" or c == LAST else "c"


def maxes(att, c, hg):
    return [("max", att, c, hg, u) for u in range(len(units(att, c)))] + [("row", att, c, hg)]


def exps(att, c, hg):
    return [("exp", att, c, hg, g, h) for g in groups(att, c) for h in heads(g)]


def project(kind, c, f):
    return [("proj", kind, c, f), ("place", kind, c, f)]


def norm(name, c):
    return [("stats", name, c, 0), ("stats", name, c, 1), ("tr", name, c, 0), ("tr", name, c, 1)]


def out_norm(att, name, c):
    return [("tr", "oT_" + att, c, 0), ("tr", "oT_" + att, c, 1), ("wo", att, c, 0), ("stats", name, c, 0),
            ("wo", att, c, 1), ("stats", name, c, 1), ("tr", name, c, 0), ("tr", name, c, 1)]


def post_norm(att, name, c):
    s = out_norm(att, name, c)
    return s[:2] + [("reload", c)] + s[2:]


def cross(att, c):
    return ([s for f in range(KT) for s in project("q" + att, c, f)]
            + [s for hg in range(NHG) for s in exps(att, c, hg)])


def mlp(l, c):
    out = [("up", l, c, 0)]
    for m in range(1, NM):
        out += [("up", l, c, m), ("down", l, c, m - 1)]
    return out + [("down", l, c, NM - 1)] + [("res", l, c, g) for g in range(NT // 2)]


def post(c):
    return (post_norm("sa", "ln2", c) + cross("ca", c) + out_norm("ca", "ln3", c)
            + mlp(0, c) + [("tr", "x3", c, g) for g in range(NT // 2)] + cross("la", c)
            + [("addatt", c, g) for g in range(NT // 2)] + norm("ln4", c) + [("lnout", c)] + mlp(1, c)
            + [("store", c)])


def prologue(c):
    return ([("load", c)] + norm("ln1", c) + [s for f in range(KT) for s in project("ks", c, f)]
            + [("v", c, g) for g in range(NT // 2)])


def context():
    return ([("ctxv", l, b) for l in range(2) for b in range(B)]
            + [("ctxk", l, f) for l in range(2) for f in range(KT)] + [("late",)])


COST = {
    "load": (("dma", 0.7),), "reload": (("dma", 0.7),), "store": (("dma", 0.7),), "late": (("dma", 1.3),),
    "stats": (("dve", 4.5),), "tr": (("pe", 0.6), ("act", 0.95)),
    "proj": (("pe", 1.9), ("act", 0.6), ("dve", 4.0)), "place": (("dma", 3.8),),
    "v": (("pe", 2.2), ("act", 0.55)), "wo": (("pe", 2.1), ("dve", 0.65)),
    "up": (("pe", 1.8), ("act", 0.6)), "down": (("pe", 1.78),), "res": (("dve", 0.65),),
    "max": (("pe", 0.3), ("dve", 0.62)), "row": (("pe", 0.15), ("dve", 0.6), ("dma", 1.3)),
    "exp": (("pe", 0.25), ("act", 0.5)), "pv": (("pe", 1.0),), "evac": (("act", 0.5),),
    "turn": (("pe", 0.5), ("dve", 0.6)), "addatt": (("dve", 0.65),), "lnout": (("pool", 5.6),),
    "ctxk": (("pe", 1.3), ("act", 0.6), ("dve", 3.5), ("dma", 3.8)), "ctxv": (("pe", 3.2), ("act", 0.7)),
}
DMA_LATENCY = 2.2
START = 4.0
CTX_LOADED = 22.0
LATENCY = 0.15

PRO, POST, CMAX, SMAX, SEXP, PV, TURN, POSTL, CMAXL, CTX = range(10)
PRIORITY = (6, 4, 1, 7, 8, 5, 3, 2, 0, 9)
CHUNK_PRIORITY = {0: (3, 4), 1: (3, 4), LAST: (1.5, -2)}
SLACK = (0.0, 0.0, 0.0, 0.0, 0.0, 0.0, 0.1, 0.1, 0.6, 0.0)
AHEAD = 4.0


def cross_maxes(chunks):
    return [s for c in chunks for att in ("ca", "la") for hg in range(NHG) for s in maxes(att, c, hg)]


def order():
    chunks = range(NCHUNK)
    threads = [[s for c in chunks for s in prologue(c)],
               [s for c in chunks if c < LAST for s in post(c)],
               cross_maxes(chunks[:LAST]),
               [s for c in chunks for f in range(KT)
                for s in project("qs", c, f) + [m for hg in (2 * f, 2 * f + 1) for m in maxes("sa", c, hg)]],
               [s for c in chunks for hg in range(NHG) for s in exps("sa", c, hg)], [], [],
               post(LAST), cross_maxes([LAST]), context()]
    at = [0] * len(threads)
    out, gelu = [], False
    fin, release = {}, {}
    free = {"pe": 0.0, "dve": 0.0, "act": 0.0, "pool": 0.0, "dma": START}
    rings = {"max": [], "exp": [], "chain": [], "misc": [], "proj": [], "q": [], "c": []}
    item = hidden = None

    def ring(s):
        k = s[0]
        if k in ("ctxk", "ctxv", "tr", "proj", "v", "wo"):
            return "chain", 2
        if k in ("row", "turn", "up"):
            return "misc", 1
        return (k, 2) if k in ("max", "exp") else (None, 0)

    def last_exp(c, hg):
        return ("exp", "sa", c, hg, groups("sa", c)[-1], HG - 1)

    def before(s):
        k = s[0]
        w = []
        if k == "load" and s[1]:
            w.append(("tr", "ln1", s[1] - 1, NT // 2 - 1))
        elif k == "reload" and s[1]:
            w.append(("tr", "ln1", LAST, NT // 2 - 1) if s[1] == LAST else ("store", s[1] - 1))
        elif k == "stats":
            _, name, c, g = s
            w.append({"ln1": ("load", c), "ln2": ("wo", "sa", c, g), "ln3": ("wo", "ca", c, g),
                      "ln4": ("addatt", c, g)}[name])
            if name == "ln2" and c == 0:
                w.append(("late",))
        elif k == "tr":
            _, what, c, g = s
            if what in NORMS:
                w.append(("stats", what, c, 1))
            elif what == "x3":
                w.append(("res", 0, c, g))
            else:
                w.append(("turn", what[3:], c, NHG - 1))
            if what == "ln1" and c:
                w.append(("proj", "qs", c - 1, KT - 1))
        elif k == "proj":
            _, kind, c, f = s
            what = {"qs": "ln1", "ks": "ln1", "qca": "ln2", "qla": "x3"}[kind]
            w += [("tr", what, c, g) for g in range(NT // 2)]
            if s[1:] == ("ks", 0, 1):
                w.append(("proj", "qs", 0, 0))
            if c and (kind == "qs" or kind == "ks" and c % 2 == 0):
                w.append(last_exp(c - 1, 2 * f + 1))
        elif k == "place":
            w.append(("proj", *s[1:]))
        elif k == "v":
            w += [("tr", "ln1", s[1], s[2])]
            if s[1] and s[1] % 2 == 0:
                w.append(("evac", "sa", s[1] - 1, NHG - 1))
        elif k == "wo":
            w.append(("tr", "oT_" + s[1], s[2], s[3]))
        elif k == "ctxk":
            w.append(("place", "qs", 0, 1))
        elif k == "ctxv":
            w.append(("proj", "ks", 0, 0))
        elif k == "up":
            w += [("tr", ("ln3", "ln4")[s[1]], s[2], g) for g in range(NT // 2)]
        elif k == "down":
            w.append(("up", *s[1:]))
        elif k == "res":
            w.append(("down", s[1], s[2], NM - 1))
            if s[1]:
                w.append(("lnout", s[2]))
        elif k == "max":
            _, att, c, hg, u = s
            f = hg // 2
            w += [("place", "qs", c, f), ("place", "ks", c, f)] if att == "sa" else \
                [("place", "q" + att, c, f), ("late",)]
        elif k == "row":
            w.append(("max", *s[1:], len(units(*s[1:3])) - 1))
        elif k == "exp":
            _, att, c, hg, g, h = s
            w.append(("row", att, c, hg))
            if att == "sa" and c:
                w.append(("tr", "oT_sa", c - 1, 1))
        elif k == "pv":
            _, att, c, hg, g = s
            w.append(("exp", *s[1:], heads(g)[-1]))
            if att == "sa":
                w += [("v", c, i) for i in range(NT // 2)]
        elif k == "turn":
            w.append(("evac", *s[1:]))
        elif k == "addatt":
            w.append(("turn", "la", s[1], NHG - 1))
        elif k == "lnout":
            w.append(("stats", "ln4", s[1], 1))
        elif k == "store":
            w += [("res", 1, s[1], g) for g in range(NT // 2)]
        return w

    pvs, evacs, exp_groups = [], [], 0

    def ready(i, s):
        k = s[0]
        if hidden not in (None, i) and k in ("exp", "up"):
            return None
        if k == "exp":
            if item not in (None, i) or s[5] == 0 and len(pvs) < exp_groups - 1:
                return None
        if k in ("proj", "ctxk") and len(rings["proj"]) >= 2:
            p = rings["proj"][-2]
            if p[0] == "proj" and ("place", *p[1:]) not in fin:
                return None
        q = side(s[1], s[2]) if k == "row" else None
        if k == "row" and len(rings[q]) >= NROW[q]:
            old = rings[q][-NROW[q]]
            if ("exp", *old[1:], groups(*old[1:3])[0], 0) not in fin:
                return None
        if k == "evac" and len(evacs) and ("turn", *evacs[-1][1:]) not in fin:
            return None
        t = CTX_LOADED if k == "ctxv" else 0.0
        for w in before(s):
            if w not in fin:
                return None
            t = max(t, fin[w])
        if k in ("proj", "ctxk") and len(rings["proj"]) >= 2:
            p = rings["proj"][-2]
            t = max(t, fin[("place", *p[1:]) if p[0] == "proj" else p] - AHEAD)
        name, n = ring(s)
        if n and len(rings[name]) >= n:
            t = max(t, release.get(rings[name][-n], 0.0))
        return t

    while any(at[i] < len(threads[i]) for i in range(10)):
        best = None
        for i in range(10):
            if at[i] == len(threads[i]):
                continue
            s = threads[i][at[i]]
            t = ready(i, s)
            if t is None:
                continue
            prio = PRIORITY[i]
            if i in (SMAX, SEXP) and s[2] in CHUNK_PRIORITY:
                prio = CHUNK_PRIORITY[s[2]][i - SMAX]
            key = (max(t - free["pe"] - SLACK[i], 0.0), prio)
            if best is None or key < best[0]:
                best = (key, i, s, t)
        assert best, "no step can stand next"
        _, i, s, t = best
        at[i] += 1
        out.append(s)
        k = s[0]
        width = 1.0
        if k in ("exp", "pv") and s[1] == "sa":
            width = 1 - max(s[4] - NT * (s[2] % 2), 0) / NT
        for j, (eng, dt) in enumerate(COST[k]):
            if k == "proj" and eng == "dve" and s[1] == "qla":
                dt = dt / 3
            elif k == "stats" and s[3] == 0:
                dt = 0.7
            elif k == "up" and eng == "act" and s[3] == 0:
                dt += 1.3
            elif k == "exp" and eng == "act" and gelu:
                dt += 1.3
            dt *= width if eng == "pe" else 0.25 + 0.75 * width
            t = free[eng] = max(free[eng], t) + dt
            t += LATENCY
            if j == 1:
                release[s] = t
        if k in ("exp", "up"):
            gelu = k == "up"
        if COST[k][-1][0] == "dma":
            t += DMA_LATENCY
        fin[s] = t
        name, n = ring(s)
        if n:
            rings[name].append(s)
        if k in ("proj", "ctxk"):
            rings["proj"].append(s)
        if k == "row":
            rings[side(s[1], s[2])].append(s)
        if k == "exp":
            item = i
            _, att, c, hg, g, h = s
            if h == heads(g)[-1]:
                exp_groups += 1
                threads[PV].append(("pv", att, c, hg, g))
                if g == groups(att, c)[-1]:
                    threads[PV].append(("evac", att, c, hg))
                    item = None
        elif k == "pv":
            pvs.append(s)
        elif k == "evac":
            evacs.append(s)
            threads[TURN].append(("turn", *s[1:]))
        elif k == "up":
            hidden = i
        elif k == "res" and s[3] == NT // 2 - 1:
            for g in range(NT // 2):
                release["res", s[1], s[2], g] = fin["res", s[1], s[2], g]
            hidden = None
            rings["exp"] += [("res", s[1], s[2], g) for g in range(NT // 2)]
    return out


def build(nc, x, ctxT, sq, fcw, cols, rows, lnrow, ident, masks, trig, out):
    ORDER = order()
    nth, seen = {}, {}
    for s in ORDER:
        seen[s[0]] = seen.get(s[0], 0) + 1
        assert s not in nth, s
        nth[s] = seen[s[0]]
    chain_use, misc_use = {}, {}
    for s in ORDER:
        if s[0] in ("ctxk", "ctxv", "tr", "proj", "v", "wo"):
            chain_use[s] = len(chain_use)
        if s[0] in ("row", "turn", "up"):
            misc_use[s] = len(misc_use)
    with ExitStack() as ctx:
        def sb(name, shape, dt=F32):
            return ctx.enter_context(nc.sbuf_tensor(name, shape, dt))

        def psum(name):
            return ctx.enter_context(nc.psum_tensor(name, [P, 512], F32))

        def sem(name):
            return ctx.enter_context(nc.semaphore(name))

        w_sq = {n: sb("w_" + n, [P, KT, E]) for n in ("sa_wq", "sa_wk", "sa_wv", "sa_wo", "ca_wq", "ca_wo", "l1_wq")}
        w_up = [sb(f"w_up{l}", [P, KT, FF]) for l in range(2)]
        w_down = [sb(f"w_down{l}", [P, NM, E]) for l in range(2)]
        col = sb("col", [P, NCOLS])
        g4b4 = sb("g4b4", [P, 2, E])
        idf = sb("idf", [P, P])
        idb = sb("idb", [P, P], BF16)
        mask = sb("mask", [P, MASKW], BF16)
        maskw, maskt, maskb = mask[:, 0:2 * P], mask[:, 2 * P:3 * P], mask[:, 3 * P:5 * P]
        cosT = sb("cosT", [P, LX])
        sinT = sb("sinT", [P, LX])
        ones3 = sb("ones3", [3, P], BF16)
        bias3 = sb("bias3", [3, len(BIAS_ROWS), E], BF16)

        KA = sb("KA", [SROW + 2, 2, H, CH], BF16)
        QA = sb("QA", [SROW + 2, H, CH], BF16)
        QC = sb("QC", [SROW + 2, H, CH], BF16)
        KC = sb("KC", [SROW + 2, 2, H, B, LYP], BF16)
        V = sb("V", [P, 2, NT, H, HD + 1])
        VA = sb("VA", [P, 2, B, H, HD + 1])
        VB = sb("VB", [P, 2, B, NHG, HD + 1])
        probs = sb("probs", [P, 2, HG, CH])
        mcol = sb("mcol", [P, sum(NROW.values()), 2, HG, NT])
        mrow = sb("mrow", [HG * NT, sum(NROW.values()), 2, P], BF16)
        osb = sb("osb", [P, CH])
        rec = sb("rec", [P, 2, NT, HG])
        a_sa = sb("a_sa", [P, NT, E])
        a_ctx = sb("a_ctx", [P, NT, E])

        xb = sb("xb", [P, 2, NT, E])
        hT = sb("hT", [P, 2, KT, CH])
        hid = sb("hid", [P, 2, CH])
        rot = sb("rot", [P, 2, CH])
        swap = sb("swap", [P, CH])
        part = sb("part", [P, 2, 3, CH], BF16)
        st6 = sb("st6", [P, 3, NT, 6])
        mv = sb("mv", [P, 3, NT, 2])
        nw = sb("nw", [P, 4, NT])

        def x_of(c):
            return xb[:, int(c == LAST)]

        def hT_of(what, c):
            return hT[:, 0 if what == "ln1" or c == LAST else 1]

        def a_of(att, c):
            return a_sa if att == "sa" or c == LAST else a_ctx

        def q_of(att, c):
            return QA if att == "sa" or c == LAST else QC

        w_ctx = w_down[1][:, :, :].rearrange("p (n k) e -> p n k e", k=KT)
        cT = a_ctx[:, :, :].rearrange("p a b -> p (a b)")[:, 0:KT * B * LY].rearrange("p (k n) -> p k n", k=KT)
        maskf = rot[:, :, :].rearrange("p a b -> p (a b)")[:, 0:MASKW]
        brow = w_up[1][0:len(BIAS_ROWS), 0, 0:E]
        bpart = [QC[0:len(BIAS_ROWS), i, 0:E] for i in range(3)]

        ps_max = [psum(f"ps_max{i}") for i in range(2)]
        ps_exp = [psum(f"ps_exp{i}") for i in range(2)]
        ps_o = psum("ps_o")
        ps_misc = psum("ps_misc")
        ps_chain = [psum(f"ps_chain{i}") for i in range(2)]

        s_ident_in, s_trig_in, s_cols = sem("ident_in"), sem("trig_in"), sem("cols_in")
        s_mask_in, s_rows_in = sem("mask_in"), sem("rows_in")
        s_wctxk = sem("wctxk_in")
        s_wctx, s_wqkv, s_wrest, s_wlate = sem("wctx_in"), sem("wqkv_in"), sem("wrest_in"), sem("wlate_in")
        s_x, s_again = sem("x_in"), [sem(f"x_in_again{i}") for i in range(2)]
        s_stored = [sem(f"stored{i}") for i in range(2)]
        s_ones, s_ones_moved = sem("ones_set"), sem("ones_moved")
        s_mask = sem("mask_ready")
        s_bpart, s_bmove = sem("bias_parts_ready"), sem("bias_parts_moved")
        s_chain_ready = sem("chain_ready")
        s_chain_free = [sem(f"chain_read{i}") for i in range(2)]
        s_misc_ready, s_misc_free = sem("misc_ready"), sem("misc_read")
        s_max_ready, s_max_done = sem("max_ready"), sem("max_done")
        s_both = sem("two_halves_max")
        s_exp_ready, s_exp_done = sem("exp_ready"), sem("exp_done")
        s_pv, s_evac = sem("pv_done"), sem("o_evacuated")
        s_mput = [sem(f"mrow_placed{i}") for i in range(sum(NROW.values()))]
        s_xn = sem("xn_ready")
        s_part = [sem(f"part{i}_ready") for i in range(3)]
        s_put = {k: [sem(f"placed_{k}{f}") for f in range(KT)] for k in ("qs", "ks", "qc", "kc")}
        s_sum_ready, s_sum_read = sem("mlp_sum_ready"), sem("mlp_sum_read")
        s_scaled = sem("q_weights_scaled")
        s_lnout = sem("ln4_written")
        s_dve, s_pool = sem("dve_chain"), sem("pool_chain")
        block = ctx.enter_context(nc.Block())

        def c0(name, i=0):
            return col[:, COLS[name][0] + i:COLS[name][0] + i + 1]

        def after_chain(eng, s):
            eng.wait_ge(s_chain_free[chain_use[s] % 2], chain_use[s] // 2 + 1)

        def after_misc(eng, s):
            eng.wait_ge(s_misc_free, misc_use[s] + 1)

        def operand(s):
            if s[0] == "ctxk":
                return "kc", s[2]
            return (s[1] if s[1] in ("qs", "ks") else "qs" if s[2] == LAST else "qc"), s[3]

        proj_nth, put_nth, both_nth, exp_nth, put_count = {}, {}, {}, {}, {}
        item_slot, item_round, rows_of = {}, {}, {"q": 0, "c": 0}
        for s in ORDER:
            if s[0] in ("proj", "ctxk"):
                proj_nth[s] = len(proj_nth) + 1
                put_count[operand(s)] = put_count.get(operand(s), 0) + 1
                put_nth[s] = put_count[operand(s)]
            elif s[0] == "row":
                q = side(s[1], s[2])
                rows_of[q] += 1
                n = NROW[q]
                item_slot[s[1:]] = rows_of[q] % n + (NROW["q"] if q == "c" else 0)
                item_round[s[1:]] = (rows_of[q] - 1) // n + 1
                if s[1] == "sa" and s[2] % 2:
                    both_nth[s[1:]] = len(both_nth) + 1
            elif s[0] == "exp":
                exp_nth[s] = len(exp_nth) + 1
        last_exp, latest = {}, {}
        for s in ORDER:
            if s[0] == "exp":
                _, att, c, hg, g, h = s
                latest["qs" if att == "sa" or c == LAST else "qc", hg // 2] = exp_nth[s]
                if att == "sa":
                    latest["ks", hg // 2, g // NT] = exp_nth[s]
            elif s[0] == "place":
                _, kind, c, f = s
                key = ("ks", f, c % 2) if kind == "ks" else (operand(s)[0], f)
                last_exp[s] = latest.get(key)
        xn_count = {s[1:3]: 2 * i for i, s in enumerate(s for s in ORDER if s[0] == "stats" and s[3] == 1)}
        exps_before, sums_before, n_exp, n_sum = {}, {}, 0, 0
        for s in ORDER:
            exps_before[s], sums_before[s] = n_exp, n_sum
            n_exp += s[0] == "exp"
            n_sum += s[0] == "res"
            exps_before["down", n_sum] = n_exp if s[0] == "res" else exps_before.get(("down", n_sum))
        projs = sorted(proj_nth, key=proj_nth.get)

        def placed(eng, s):
            key, f = operand(s)
            eng.wait_ge(s_put[key][f], 16 * NPROD * put_nth[s])

        @block.sync
        def _(sp):
            def chunk_of(a, c):
                return a[c // 2, (c % 2) * CH:(c % 2 + 1) * CH, :].rearrange("(t p) e -> p t e", p=P)

            sp.dma_start(xb[:, 1, :, :], chunk_of(x, 0)).then_inc(s_x, 16)
            sp.dma_start(brow, rows).then_inc(s_rows_in, 16)
            sp.dma_start(idf[:, :], ident).then_inc(s_ident_in, 16)
            sp.dma_start(col[:, :], cols).then_inc(s_cols, 16)
            sp.dma_start(maskf, masks).then_inc(s_mask_in, 16)
            for n in ("sa_wk", "sa_wq", "sa_wv"):
                sp.dma_start(w_sq[n][:, :, :], sq[n]).then_inc(s_wqkv, 16)
            sp.dma_start(cosT[:, :], trig[0]).then_inc(s_trig_in, 16)
            sp.dma_start(sinT[:, :], trig[1]).then_inc(s_trig_in, 16)
            sp.dma_start(cT, ctxT).then_inc(s_wctx, 16)
            for i, n in ((1, "ca_wv"), (3, "l1_wv")):
                sp.dma_start(w_ctx[:, i], sq[n]).then_inc(s_wctx, 16)
            for i, n in ((0, "ca_wk"), (2, "l1_wk")):
                sp.dma_start(w_ctx[:, i], sq[n]).then_inc(s_wctxk, 16)
            sp.wait_ge(s_ones, 1)
            ones = KA[SROW:SROW + 2, 0, :, :]
            sp.dma_start(KA[SROW:SROW + 2, 1, :, :], ones).then_inc(s_ones_moved, 16)
            for l in range(2):
                for b in range(B):
                    sp.dma_start(KC[SROW:SROW + 2, l, :, b, :], ones[:, :, 0:LYP]).then_inc(s_ones_moved, 16)
            for n in ("sa_wo", "ca_wq", "ca_wo", "l1_wq"):
                sp.dma_start(w_sq[n][:, :, :], sq[n]).then_inc(s_wrest, 16)
            sp.dma_start(w_up[0][:, :, :], fcw[0]).then_inc(s_wrest, 16)
            sp.dma_start(w_down[0][:, :, :], fcw[1]).then_inc(s_wrest, 16)
            sp.dma_start(g4b4[:, :, :], lnrow).then_inc(s_wrest, 16)
            sp.wait_ge(s_bpart, 3)
            for i in range(3):
                sp.dma_start(bias3[i:i + 1, :, :], bpart[i]).then_inc(s_bmove, 16)
            for s in ORDER:
                k = s[0]
                if k == "load" and s[1] > 0:
                    c = s[1]
                    sp.wait_ge(s_chain_ready, chain_use[("tr", "ln1", c - 1, NT // 2 - 1)] + 1)
                    sp.dma_start(xb[:, 1, :, :], chunk_of(x, c)).then_inc(s_x, 16)
                elif k == "reload":
                    c = s[1]
                    if c == LAST:
                        sp.wait_ge(s_chain_ready, chain_use[("tr", "ln1", c, NT // 2 - 1)] + 1)
                    elif c:
                        sp.wait_ge(s_stored[0], 16 * c)
                    sp.dma_start(x_of(c), chunk_of(x, c)).then_inc(s_again[int(c == LAST)], 16)
                elif k == "late":
                    after_chain(sp, ("ctxk", 1, KT - 1))
                    sp.dma_start(w_up[1][:, :, :], fcw[2]).then_inc(s_wlate, 16)
                    sp.dma_start(w_down[1][:, :, :], fcw[3]).then_inc(s_wlate, 16)
                elif k in ("place", "ctxk"):
                    p = s if k == "ctxk" else ("proj", *s[1:])
                    key, f = operand(p)
                    n = proj_nth[p]
                    which = QPART if key in ("qs", "qc") else KPART
                    if k == "place" and last_exp[s]:
                        sp.wait_ge(s_exp_done, last_exp[s])
                    if key == "qc":
                        sp.wait_ge(s_bmove, 48)
                    for i in range(3):
                        sp.wait_ge(s_part[i], n)
                        for g in range(NPROD):
                            if which[g] != i:
                                continue
                            rows_g = slice(g * HD, (g + 1) * HD)
                            hs = slice(f * HH, (f + 1) * HH)
                            if k == "ctxk":
                                sp.dma_start(
                                    KC[rows_g, s[1], hs, :, 0:LY].rearrange("r h b n -> r (h b) n"),
                                    part[:, n % 2, i, 0:B * LY].rearrange("p (b n) -> p b n", b=B),
                                ).then_inc(s_put[key][f], 16)
                            else:
                                dst = {"qs": QA, "ks": KA[:, s[2] % 2], "qc": QC}[key][rows_g, hs, :]
                                sp.dma_start(dst, part[:, n % 2, i, :]).then_inc(s_put[key][f], 16)
                elif k == "row":
                    _, att, c, hg = s
                    n = item_slot[s[1:]]
                    after_misc(sp, s)
                    q, h0 = q_of(att, c), hg * HG
                    for i in range(2):
                        sp.dma_start(q[SROW + i:SROW + i + 1, h0:h0 + HG, :],
                                     mrow[:, n, i, :]).then_inc(s_mput[n], 16)
                elif k == "store":
                    c = s[1]
                    sp.wait_ge(s_sum_read, nth[("res", 1, c, NT // 2 - 1)])
                    sp.dma_start(chunk_of(out, c), x_of(c)).then_inc(s_stored[int(c == LAST)], 16)
            sp.wait_ge(s_stored[0], 16 * LAST)
            sp.wait_ge(s_stored[1], 16)

        @block.tensor
        def _(pe):
            pe.wait_ge(s_ident_in, 16)
            n_max = [0]

            def chain_bank(s):
                n = chain_use[s]
                if n >= 2:
                    pe.wait_ge(s_chain_free[n % 2], n // 2)
                return ps_chain[n % 2]

            def misc_bank(s):
                n = misc_use[s]
                if n >= 1:
                    pe.wait_ge(s_misc_free, n)
                return ps_misc

            waited = set()

            def once(key, s, v):
                if key not in waited:
                    waited.add(key)
                    pe.wait_ge(s, v)

            def add_bias(dst, name, m=P, start=True):
                once("bias", s_bmove, 48)
                once("mask", s_mask, 3)
                i = BIAS_ROWS.index(name)
                pe.matmul(dst, ones3[0:3, 0:m], bias3[0:3, i, :], start=start, stop=False, skip_group_check=True)

            for s in ORDER:
                k = s[0]
                if k == "ctxk":
                    _, l, f = s
                    once("wctxk", s_wctxk, 32)
                    bank = chain_bank(s)
                    for t in range(KT):
                        mm = pe.matmul(bank[:, 0:B * LY], w_ctx[:, 2 * l, t, f * P:(f + 1) * P], cT[:, t, :],
                                       start=(t == 0), stop=(t == KT - 1))
                    mm.then_inc(s_chain_ready, 1)
                elif k == "ctxv":
                    _, l, b = s
                    once("wctx", s_wctx, 48)
                    bank = chain_bank(s)
                    name = ("ca_bv", "l1_bv")[l]
                    add_bias(bank[:, 0:E], name)
                    for t in range(KT):
                        pe.matmul(bank[:, 0:E], cT[:, t, b * LY:b * LY + P], w_ctx[:, 2 * l + 1, t, :],
                                  start=False, stop=(t == KT - 1), skip_group_check=True)
                    for j in range(HG):
                        dst = bank[32 * j:32 * j + LYB, E:2 * E]
                        add_bias(dst, name, LYB, start=False)
                        for t in range(KT):
                            mm = pe.matmul(dst, cT[:, t, b * LY + P:(b + 1) * LY], w_ctx[:, 2 * l + 1, t, :],
                                           start=False, stop=(t == KT - 1), skip_group_check=True)
                    mm.then_inc(s_chain_ready, 1)
                elif k == "tr":
                    _, what, c, g = s
                    if what in NORMS:
                        pe.wait_ge(s_xn, xn_count[what, c] + g + 1)
                        src = xb[:, 1] if what == "ln1" else a_of(what, c)
                    elif what == "x3":
                        pe.wait_ge(s_sum_read, nth[("res", 0, c, g)])
                        src = x_of(c)
                    else:
                        att = what[3:]
                        after_misc(pe, ("turn", att, c, NHG - 1))
                        src = a_of(att, c)
                    bank = chain_bank(s)
                    for f in range(KT):
                        for t in range(2):
                            mm = pe.transpose(bank[:, (2 * f + t) * P:(2 * f + t + 1) * P],
                                              src[:, 2 * g + t, f * P:(f + 1) * P], idf[:, :])
                    mm.then_inc(s_chain_ready, 1)
                elif k in ("proj", "v", "wo"):
                    what = "ln1" if k == "v" or (k == "proj" and s[1] in ("qs", "ks")) else None
                    if k == "v":
                        name, c = "sa_wv", s[1]
                    elif k == "wo":
                        name, c = s[1] + "_wo", s[2]
                        what = "oT_" + s[1]
                    else:
                        name, c = {"qs": "sa_wq", "ks": "sa_wk", "qca": "ca_wq", "qla": "l1_wq"}[s[1]], s[2]
                        what = what or {"qca": "ln2", "qla": "x3"}[s[1]]
                    once("wqkv", s_wqkv, 48)
                    if what != "ln1":
                        once("wrest", s_wrest, 16 * 7)
                    for g in range(NT // 2):
                        if k == "proj" or g == s[-1]:
                            after_chain(pe, ("tr", what, c, g))
                    src = hT_of(what, c)
                    w = w_sq[name]
                    if name.endswith("_wq"):
                        once(name, s_scaled, {"sa_wq": 4, "ca_wq": 5, "l1_wq": 6}[name])
                    bank = chain_bank(s)
                    if k == "proj":
                        f = s[3]
                        for t in range(KT):
                            mm = pe.matmul(bank[:, :], w[:, t, f * P:(f + 1) * P], src[:, t, :],
                                           start=(t == 0), stop=(t == KT - 1))
                    else:
                        for i in range(2):
                            dst = bank[:, i * E:(i + 1) * E]
                            add_bias(dst, "sa_bv" if k == "v" else s[1] + "_bo")
                            tok = (2 * s[-1] + i) * P
                            for t in range(KT):
                                mm = pe.matmul(dst, src[:, t, tok:tok + P], w[:, t, :],
                                               start=False, stop=(t == KT - 1), skip_group_check=True)
                    mm.then_inc(s_chain_ready, 1)
                elif k == "up":
                    _, l, c, m = s
                    for g in range(NT // 2):
                        after_chain(pe, ("tr", ("ln3", "ln4")[l], c, g))
                    if l:
                        once("wlate", s_wlate, 32)
                    elif m == 0:
                        once("wrest", s_wrest, 16 * 7)
                    bank = misc_bank(s)
                    for t in range(KT):
                        mm = pe.matmul(bank[:, :], w_up[l][:, t, m * P:(m + 1) * P], hT_of("up", c)[:, t, :],
                                       start=(t == 0), stop=(t == KT - 1))
                    mm.then_inc(s_misc_ready, 1)
                elif k == "down":
                    _, l, c, m = s
                    if m == 0:
                        if exps_before[s]:
                            pe.wait_ge(s_exp_done, exps_before[s])
                        if sums_before[s]:
                            pe.wait_ge(s_sum_read, sums_before[s])
                    after_misc(pe, ("up", l, c, m))
                    for t in range(NT):
                        dst = ps_exp[t // 2][:, (t % 2) * E:(t % 2 + 1) * E]
                        if m == 0:
                            add_bias(dst, ("fc2_b", "l1_b2")[l], start=(t % 2 == 0))
                        mm = pe.matmul(dst, hid[:, m % 2, t * P:(t + 1) * P], w_down[l][:, m, :],
                                       start=False, stop=(m == NM - 1), skip_group_check=True)
                        if m == NM - 1 and t % 2:
                            mm.then_inc(s_sum_ready, 1)
                elif k == "max":
                    _, att, c, hg, u = s
                    unit = units(att, c)[u]
                    once("mask", s_mask, 3)
                    if (att, c) != ("sa", 0):
                        once("ones", s_ones, 2)
                        once("ones_moved", s_ones_moved, 16 * (1 + 2 * B))
                    if u == 0:
                        f = hg // 2
                        if att == "sa":
                            placed(pe, ("proj", "qs", c, f))
                            placed(pe, ("proj", "ks", c, f))
                        else:
                            placed(pe, ("proj", "q" + att, c, f))
                            once(("kc", f), s_put["kc"][f], 16 * NPROD * 2)
                    if n_max[0] >= 2:
                        pe.wait_ge(s_max_done, n_max[0] - 1)
                    bank = ps_max[n_max[0] % 2]
                    n_max[0] += 1
                    for t, h, half, n, pt, at0 in unit:
                        dst = bank[:, at0:at0 + n]
                        if att == "sa":
                            q = QA[0:SROW, hg * HG + h, t * P:(t + 1) * P]
                            kk = KA[0:SROW, half, hg * HG + h, 0:n]
                            causal = [(n - P, P, maskw[:, 0:P])] if pt == 0 else []
                        else:
                            l = int(att == "la")
                            q = q_of(att, c)[0:SROW, hg * HG + h, t * P:(t + 1) * P]
                            kk = KC[0:SROW, l, hg * HG + h, c // 2, 0:LY]
                            causal = []
                            if l and c % 2 == 0 and t < 2:
                                causal = [[(0, LY, maskw[:, 0:LY])], [(P, LYB, maskw[:, 0:LYB])]][t]
                        mm = pe.matmul(dst, q, kk, start=True, stop=not causal)
                        for a0, w0, mk in causal:
                            mm = pe.matmul(bank[:, at0 + a0:at0 + a0 + w0], idb[:, :], mk, start=False, stop=True)
                    mm.then_inc(s_max_ready, 1)
                elif k == "row":
                    n = item_slot[s[1:]]
                    _, att, c, hg = s
                    if s[1:] in both_nth:
                        pe.wait_ge(s_both, both_nth[s[1:]])
                    else:
                        pe.wait_ge(s_max_done, nth[("max", att, c, hg, len(units(att, c)) - 1)])
                    bank = misc_bank(s)
                    src = mcol[:, n, 0, :, :].rearrange("p h t -> p (h t)")
                    pe.transpose(bank[0:NT * HG, 0:P], src, idf[:, :]).then_inc(s_misc_ready, 1)
                elif k == "exp":
                    _, att, c, hg, g, h = s
                    once("ones0", s_ones, 1)
                    if g == groups(att, c)[0] and h == 0:
                        n = item_slot[(att, c, hg)]
                        pe.wait_ge(s_mput[n], 32 * item_round[(att, c, hg)])
                    n = exp_nth[s]
                    if n > 2:
                        pe.wait_ge(s_exp_done, n - 2)
                    if sums_before[s] and n - exps_before["down", sums_before[s]] <= 2:
                        pe.wait_ge(s_sum_read, sums_before[s])
                    bank = ps_exp[n % 2]
                    l = int(att == "la")
                    hh = hg * HG + h
                    causal = l and c % 2 == 0
                    if att == "sa":
                        r = g - NT * (c % 2)
                        q0 = max(r, 0) * P
                        mm = pe.matmul(bank[:, q0:CH], KA[:, g // NT, hh, (g % NT) * P:(g % NT + 1) * P],
                                       QA[:, hh, q0:CH], start=True, stop=(r < 0))
                        if r >= 0:
                            mm = pe.matmul(bank[:, q0:q0 + P], idb[:, :], maskt, start=False, stop=True)
                    elif g == "A":
                        mm = pe.matmul(bank[:, :], KC[:, l, hh, c // 2, 0:P], q_of(att, c)[:, hg * HG + h, :],
                                       start=True, stop=not causal)
                        if causal:
                            mm = pe.matmul(bank[:, 0:P], idb[:, :], maskt, start=False, stop=True)
                    else:
                        for h in range(HG):
                            mm = pe.matmul(bank[32 * h:32 * h + 32, :], KC[:, l, hg * HG + h, c // 2, P:LYP],
                                           q_of(att, c)[:, hg * HG + h, :], start=True, stop=not causal,
                                           skip_group_check=True)
                        if causal:
                            mm = pe.matmul(bank[:, 0:2 * P], idb[:, :], maskb, start=False, stop=True,
                                           skip_group_check=True)
                    mm.then_inc(s_exp_ready, 1)
                elif k == "pv":
                    _, att, c, hg, g = s
                    n = nth[s]
                    pe.wait_ge(s_exp_done, exp_nth[("exp", att, c, hg, g, heads(g)[-1])])
                    first = g == groups(att, c)[0]
                    last = g == groups(att, c)[-1]
                    if first:
                        item = nth[("evac", att, c, hg)]
                        if item > 1:
                            pe.wait_ge(s_evac, item - 1)
                        if att == "sa":
                            for i in range(NT // 2):
                                after_chain(pe, ("v", c, i))
                    for h in range(HG):
                        hh = hg * HG + h
                        p0, q0 = 32 * h, 0
                        if att == "sa":
                            q0 = max(g - NT * (c % 2), 0) * P
                            v, pr = V[:, g // NT, g % NT, hh, :], probs[:, n % 2, h, q0:CH]
                        elif g == "A":
                            v, pr = VA[:, int(att == "la"), c // 2, hh, :], probs[:, n % 2, h, :]
                        else:
                            v = VB[p0:p0 + LYB, int(att == "la"), c // 2, hg, :]
                            pr = probs[p0:p0 + LYB, n % 2, 0, :]
                        mm = pe.matmul(ps_o[p0:p0 + HD + 1, q0:CH], v, pr, start=first, stop=last,
                                       skip_group_check=True)
                    mm.then_inc(s_pv, 1)
                elif k == "turn":
                    n = nth[s]
                    pe.wait_ge(s_evac, n)
                    bank = misc_bank(s)
                    for t in range(NT):
                        mm = pe.transpose(bank[:, t * P:(t + 1) * P], osb[:, t * P:(t + 1) * P], idf[:, :])
                    mm.then_inc(s_misc_ready, 1)

        @block.vector
        def _(dve):
            chain = [0]

            def link(ins):
                chain[0] += 1
                ins.then_inc(s_dve, 1)
                dve.wait_ge(s_dve, chain[0])

            for s in ORDER:
                k = s[0]
                if s == ("tr", "ln1", 0, 0):
                    dve.memset(ps_o[:, :], 0.0)
                    dve.wait_ge(s_mask_in, 16)
                    dve.tensor_copy(mask[:, :], maskf).then_inc(s_mask, 1)
                    dve.tensor_copy(idb[:, :], idf[:, :]).then_inc(s_mask, 1)
                    dve.memset(ones3[:, :], 1.0).then_inc(s_mask, 1)
                if s == ("stats", "ln1", 0, 0):
                    dve.wait_ge(s_rows_in, 16)
                    for i in range(3):
                        dve.tensor_copy(bpart[i], brow).then_inc(s_bpart, 1)
                        if i < 2:
                            dve.wait_ge(s_bpart, i + 1)
                            link(dve.tensor_tensor(brow, brow, bpart[i], ALU.subtract))
                if k in ("ctxk", "proj"):
                    n = proj_nth[s]
                    u = chain_use[s]
                    i = n % 2
                    bank = ps_chain[u % 2]
                    if k == "ctxk":
                        rope = s[1] == 0
                        pieces = [(b * LY, 0, LY) for b in range(B)]
                        width = B * LY
                    else:
                        kind, c, _ = s[1:]
                        rope = kind != "qla"
                        pieces = [(0, (c % 2) * CH, CH)]
                        width = CH
                    if n > 2:
                        placed(dve, projs[n - 3])
                    after_chain(dve, s)
                    r, w = rot[:, i, 0:width], swap[:, 0:width]
                    p1, p2 = part[:, i, 0, 0:width], part[:, i, 1, 0:width]
                    if rope:
                        if n == 1:
                            dve.wait_ge(s_trig_in, 32)
                        for a0, t0, wd in pieces:
                            for lo, hi in ((0, 64), (64, 0)):
                                ins = dve.tensor_tensor(w[lo:lo + 64, a0:a0 + wd], r[hi:hi + 64, a0:a0 + wd],
                                                        sinT[hi:hi + 64, t0:t0 + wd], ALU.mult)
                        link(ins)
                        for a0, t0, wd in pieces:
                            ins = dve.tensor_tensor(r[:, a0:a0 + wd], r[:, a0:a0 + wd], cosT[:, t0:t0 + wd], ALU.mult)
                        link(ins)
                        link(dve.tensor_tensor(r, r, w, ALU.add))
                    dve.tensor_copy(p1, r).then_inc(s_part[0], 1)
                    dve.wait_ge(s_part[0], n)
                    link(dve.tensor_tensor(r, r, p1, ALU.subtract))
                    dve.tensor_copy(p2, r).then_inc(s_part[1], 1)
                elif k == "wo" or k == "res":
                    _, _, c, g = s
                    if k == "wo":
                        u = chain_use[s]
                        dve.wait_ge(s_chain_ready, u + 1)
                        bank, read = ps_chain[u % 2], s_chain_free[u % 2]
                    else:
                        dve.wait_ge(s_sum_ready, nth[s])
                        bank, read = ps_exp[g], s_sum_read
                    if k == "res" and s[1] == 1:
                        dve.wait_ge(s_lnout, nth[("lnout", c)])
                    if k == "wo" and s[1] == "sa":
                        dve.wait_ge(s_again[int(c == LAST)], 16 if c == LAST else 16 * (c + 1))
                    xs = x_of(c)[:, 2 * g:2 * g + 2, :].rearrange("p t e -> p (t e)")
                    dve.tensor_tensor(xs, xs, bank[:, :], ALU.add).then_inc(read, 1)
                elif k == "addatt":
                    _, c, g = s
                    after_misc(dve, ("turn", "la", c, NHG - 1))
                    xs = x_of(c)[:, 2 * g:2 * g + 2, :]
                    link(dve.tensor_tensor(xs, xs, a_of("la", c)[:, 2 * g:2 * g + 2, :], ALU.add))
                elif k == "stats":
                    _, what, c, g = s
                    tiles = (2 * g, 2 * g + 1)
                    if what == "ln1":
                        dve.wait_ge(s_x, 16 * (c + 1))
                    elif what != "ln4":
                        after_chain(dve, ("wo", {"ln2": "sa", "ln3": "ca"}[what], c, g))
                    xs = xb[:, 1] if what == "ln1" else x_of(c)
                    z = 0 if what == "ln1" else 1 + int(c == LAST)
                    for t in tiles:
                        ins = dve.bn_stats(st6[:, z, t, :], xs[:, t, :])
                    if g == 0:
                        continue
                    link(ins)
                    for t in range(NT):
                        ins = dve.bn_aggr(mv[:, z, t, :], st6[:, z, t, :])
                    link(ins)
                    v, y, t1, t2 = (nw[:, i, :] for i in range(4))
                    link(dve.tensor_scalar(v, mv[:, z, :, 1], EPS, None, ALU.add))
                    link(dve.tensor_scalar(t1.bitcast(I32), v.bitcast(I32), 1, None, ALU.logical_shift_right))
                    link(dve.tensor_scalar(y.bitcast(I32), t1.bitcast(I32), -1, RSQRT_GUESS, ALU.mult, ALU.add))
                    for _ in range(3):
                        link(dve.tensor_tensor(t1, y, y, ALU.mult))
                        link(dve.scalar_tensor_tensor(t2, t1, -0.5, v, ALU.mult, ALU.mult))
                        link(dve.scalar_tensor_tensor(y, t2, 1.5, y, ALU.add, ALU.mult))
                    if what == "ln3" or what == "ln2" and c == LAST:
                        dve.wait_ge(s_chain_ready, chain_use[("tr", {"ln2": "oT_sa", "ln3": "oT_ca"}[what], c, 1)] + 1)
                    elif what == "ln2" and c > 0:
                        dve.wait_ge(s_lnout, nth[("lnout", c - 1)])
                    elif what == "ln2":
                        dve.wait_ge(s_chain_ready, chain_use[("ctxk", 1, KT - 1)] + 1)
                    dst = xs if what == "ln1" else a_of(what, c)
                    for t in range(NT):
                        ins = dve.tensor_scalar(dst[:, t, :], xs[:, t, :], mv[:, z, t, 0:1], y[:, t:t + 1],
                                                ALU.subtract, ALU.mult)
                        if t % 2:
                            ins.then_inc(s_xn, 1)
                elif k == "max":
                    _, att, c, hg, u = s
                    unit = units(att, c)[u]
                    n = item_slot[(att, c, hg)]
                    dve.wait_ge(s_max_ready, nth[s])
                    bank = ps_max[(nth[s] - 1) % 2]
                    t, h, _, w, pt, _ = unit[0]
                    step = w if att == "sa" else LYP
                    src = bank[:, 0:len(unit) * step].rearrange("p (n w) -> p n w", w=step)[:, :, 0:w]
                    if att == "sa":
                        dst = mcol[:, n, pt, h:h + len(unit), t]
                    else:
                        k0 = h * NT + t
                        dst = mcol[:, n, 0, :, :].rearrange("p h t -> p (h t)")[:, k0:k0 + len(unit)]
                    dve.tensor_reduce(dst, src, AX.X, ALU.max).then_inc(s_max_done, 1)
                elif k == "row":
                    _, att, c, hg = s
                    n = item_slot[s[1:]]
                    if s[1:] in both_nth:
                        dve.wait_ge(s_max_done, nth[("max", att, c, hg, len(units(att, c)) - 1)])
                        m0, m1 = mcol[:, n, 0, :, :], mcol[:, n, 1, :, :]
                        dve.tensor_tensor(m0, m0, m1, ALU.max).then_inc(s_both, 1)
                    dve.wait_ge(s_misc_ready, misc_use[s] + 1)
                    src = ps_misc[0:NT * HG, 0:P]
                    link(dve.tensor_scalar(mrow[:, n, 0, :], src, -1.0, None, ALU.mult))
                    dve.scalar_tensor_tensor(mrow[:, n, 1, :], src, -1.0, mrow[:, n, 0, :],
                                             ALU.mult, ALU.subtract).then_inc(s_misc_free, 1)
                elif k == "turn":
                    _, att, c, hg = s
                    n = nth[s]
                    dve.wait_ge(s_misc_ready, misc_use[s] + 1)
                    src = ps_misc[:, :].rearrange("p (t h w) -> p t h w", t=NT, h=HG)
                    r = rec[:, n % 2]
                    link(dve.reciprocal(r, src[:, :, :, HD]))
                    dst = a_of(att, c)[:, :, hg * HG * HD:(hg + 1) * HG * HD]
                    dst = dst.rearrange("p t (h d) -> p t h d", h=HG)
                    rb = r.unsqueeze(3).to_broadcast([P, NT, HG, HD])
                    dve.tensor_tensor(dst, src[:, :, :, 0:HD], rb, ALU.mult).then_inc(s_misc_free, 1)

        @block.scalar
        def _(act):
            act.wait_ge(s_cols, 16)
            turns = [s for s in ORDER if s[0] == "turn"]
            for s in ORDER:
                k = s[0]
                if k in ("tr", "v", "ctxv", "proj", "ctxk"):
                    u = chain_use[s]
                    act.wait_ge(s_chain_ready, u + 1)
                    bank = ps_chain[u % 2]
                if k == "tr":
                    _, what, c, g = s
                    dst = hT_of(what, c)[:, :, 2 * g * P:(2 * g + 2) * P]
                    src = bank[:, :].rearrange("p (f n) -> p f n", f=KT)
                    if what in NORMS:
                        for f in range(KT):
                            ins = act.activation(dst[:, f, :], src[:, f, :], ACT.Identity,
                                                 bias=c0(what + "_b", f), scale=c0(what + "_g", f))
                    else:
                        ins = act.activation(dst, src, ACT.Copy)
                    ins.then_inc(s_chain_free[u % 2], 1)
                elif k in ("proj", "ctxk"):
                    if k == "ctxk":
                        name, f, width = ("ca_bk", "l1_bk")[s[1]], s[2], B * LY
                    else:
                        name, f, width = {"qs": "sa_bq", "ks": "sa_bk", "qca": "ca_bq", "qla": "l1_bq"}[s[1]], s[3], CH
                    n = proj_nth[s]
                    if n > 2:
                        act.wait_ge(s_part[2], n - 2)
                    elif n == 1:
                        act.wait_ge(s_scaled, 3)
                        act.wait_ge(s_mask, 2)
                    act.activation(rot[:, n % 2, 0:width], bank[:, 0:width], ACT.Identity,
                                   bias=c0(name, f)).then_inc(s_chain_free[u % 2], 1)
                elif k == "v":
                    _, c, g = s
                    act.activation(V[:, c % 2, 2 * g:2 * g + 2, :, 0:HD],
                                   bank[:, :].rearrange("p (t h d) -> p t h d", t=2, h=H),
                                   ACT.Copy).then_inc(s_chain_free[u % 2], 1)
                elif k == "ctxv":
                    _, l, b = s
                    act.activation(VA[:, l, b, :, 0:HD], bank[:, 0:E].rearrange("p (h d) -> p h d", h=H), ACT.Copy)
                    for j in range(HG):
                        q = slice(32 * j, 32 * j + LYB)
                        src = bank[q, E:2 * E].rearrange("p (g h d) -> p g h d", g=NHG, h=HG)[:, :, j, :]
                        ins = act.activation(VB[q, l, b, :, 0:HD], src, ACT.Copy)
                    ins.then_inc(s_chain_free[u % 2], 1)
                elif k == "up":
                    _, l, c, m = s
                    act.wait_ge(s_misc_ready, misc_use[s] + 1)
                    act.activation(hid[:, m % 2, :], ps_misc[:, :], (ACT.Gelu_apprx_tanh, ACT.Gelu)[l],
                                   bias=c0(("fc1_b", "l1_b1")[l], m)).then_inc(s_misc_free, 1)
                elif k == "exp":
                    _, att, c, hg, g, h = s
                    n = nth[("pv", att, c, hg, g)]
                    if n > 2 and h == 0:
                        act.wait_ge(s_pv, n - 2)
                    act.wait_ge(s_exp_ready, exp_nth[s])
                    q0 = max(g - NT * (c % 2), 0) * P if att == "sa" else 0
                    act.activation(probs[:, n % 2, h, q0:CH], ps_exp[exp_nth[s] % 2][:, q0:CH],
                                   ACT.Exp).then_inc(s_exp_done, 1)
                elif k == "evac":
                    _, att, c, hg = s
                    act.wait_ge(s_pv, nth[("pv", att, c, hg, groups(att, c)[-1])])
                    if nth[s] > 1:
                        act.wait_ge(s_misc_ready, misc_use[turns[nth[s] - 2]] + 1)
                    act.activation(osb[:, :], ps_o[:, :], ACT.Copy).then_inc(s_evac, 1)

        @block.gpsimd
        def _(pool):
            chain = [0]

            def link(ins):
                chain[0] += 1
                ins.then_inc(s_pool, 1)
                pool.wait_ge(s_pool, chain[0])

            def scale(a, n):
                pool.tensor_scalar(a, a, SCALE, None, ALU.mult).then_inc(s_scaled, 1)
                pool.wait_ge(s_scaled, n)

            pool.wait_ge(s_cols, 16)
            for i, name in enumerate(("sa_bq", "ca_bq", "l1_bq")):
                scale(col[:, COLS[name][0]:COLS[name][0] + KT], i + 1)
            link(pool.memset(KA[SROW:SROW + 2, 0, :, :].bitcast(I32), TWO_ONES))
            pool.memset(V[:, :, :, :, HD:HD + 1], 1.0).then_inc(s_ones, 1)
            pool.wait_ge(s_ones, 1)
            pool.wait_ge(s_wqkv, 48)
            scale(w_sq["sa_wq"][:, :, :], 4)
            for s in ORDER:
                k = s[0]
                if s == ("place", "qs", 0, 1):
                    link(pool.memset(KC[0:SROW, :, :, :, LY:LYP], 0.0))
                    link(pool.memset(VA[:, :, :, :, HD:HD + 1], 1.0))
                    pool.memset(VB[:, :, :, :, HD:HD + 1], 1.0).then_inc(s_ones, 1)
                    pool.wait_ge(s_ones, 2)
                    pool.wait_ge(s_wrest, 16 * 7)
                    scale(w_sq["ca_wq"][:, :, :], 5)
                    scale(w_sq["l1_wq"][:, :, :], 6)
                if k in ("proj", "ctxk"):
                    n = proj_nth[s]
                    width = B * LY if k == "ctxk" else CH
                    pool.wait_ge(s_part[1], n)
                    pool.tensor_tensor(part[:, n % 2, 2, 0:width], rot[:, n % 2, 0:width],
                                       part[:, n % 2, 1, 0:width], ALU.subtract).then_inc(s_part[2], 1)
                elif k == "lnout":
                    c = s[1]
                    pool.wait_ge(s_xn, xn_count["ln4", c] + 2)
                    for i, op in enumerate((ALU.mult, ALU.add)):
                        for t in range(NT):
                            ins = pool.tensor_tensor(x_of(c)[:, t, :], (a_of("ln4", c) if i == 0 else x_of(c))[:, t, :],
                                                     g4b4[:, i, :], op)
                        if i == 0:
                            link(ins)
                    ins.then_inc(s_lnout, 1)


def rows_first(a):
    return np.ascontiguousarray(a.reshape(-1, P, a.shape[1]).transpose(1, 0, 2))


def by_head(a):
    return a.reshape(a.shape[:-1] + (KT, HH, HD)).swapaxes(-1, -2).reshape(a.shape)


def constants():
    q, k = np.arange(P)[:, None], np.arange(2 * P)[None, :]
    first = np.where(k > q, NEG, 0.0)
    second = np.where(q > k[:, :P], NEG, 0.0)
    last = np.where(P + q % 32 > k, NEG, 0.0)
    masks = np.concatenate([first, second, last], 1).astype(np.float32)
    inv = (1.0 / np.float32(10000.0) ** (np.arange(0, HD, 2, dtype=np.float32) / np.float32(HD))).astype(np.float32)
    angle = np.outer(np.arange(LX, dtype=np.float32), inv).astype(np.float32)
    row = np.arange(P) // HH
    cos = np.cos(angle).T[row % (HD // 2)]
    sin = np.sin(angle).T[row % (HD // 2)] * np.where(row < HD // 2, 1.0, -1.0)[:, None]
    return np.eye(P, dtype=np.float32), masks, np.stack([cos, sin]).astype(np.float32)


def kernel(**inputs):
    import concourse.bacc as bacc
    from concourse.bass_utils import run_bass_kernel_spmd

    a = {k: np.asarray(v) for k, v in inputs.items()}
    l0 = {k[len("L0_xattn_"):]: v for k, v in a.items() if k.startswith("L0_xattn_")}
    l1 = {k[len("L1_xattn_"):]: v for k, v in a.items() if k.startswith("L1_xattn_")}
    vec = dict(l0, l1_bq=l1["bq"], l1_bk=l1["bk"], l1_bv=l1["bv"], l1_b1=l1["b1"], l1_b2=l1["b2"],
               ln4_g=l1["ln_g"], ln4_b=l1["ln_b"])
    heads = ("sa_bq", "sa_bk", "ca_bq", "ca_bk", "l1_bq", "l1_bk")
    sq = {"sa_wq": by_head(l0["sa_wq"]), "sa_wk": by_head(l0["sa_wk"]), "sa_wv": l0["sa_wv"], "sa_wo": l0["sa_wo"],
          "ca_wq": by_head(l0["ca_wq"]), "ca_wk": by_head(l0["ca_wk"]), "ca_wv": l0["ca_wv"], "ca_wo": l0["ca_wo"],
          "l1_wq": by_head(l1["Wq"].T), "l1_wk": by_head(l1["Wk"].T), "l1_wv": l1["Wv"].T}
    ident, masks, trig = constants()
    data = {
        "x": a["x"],
        "ctxT": rows_first(np.ascontiguousarray(a["ctx_1024"].transpose(2, 0, 1)).reshape(E, B * LY)),
        **{n: rows_first(w) for n, w in sq.items()},
        "fc1": rows_first(l0["fc1_w"]), "fc2": rows_first(l0["fc2_w"]),
        "l1w1": rows_first(l1["W1"].T), "l1w2": rows_first(l1["W2"].T),
        "cols": np.concatenate([(by_head(vec[n]) if n in heads else vec[n]).reshape(k, P).T
                                for n, (_, k) in COLS.items()], 1),
        "rows": np.stack([vec[n] for n in BIAS_ROWS]),
        "lnrow": np.broadcast_to(np.stack([l1["ln_g"], l1["ln_b"]])[None], (P, 2, E)),
        "ident": ident, "masks": masks, "trig": trig,
    }
    nc = bacc.Bacc("TRN2", target_bir_lowering=False, num_devices=1, dynamic_dma_scratch_size=1024)
    data = {k: np.ascontiguousarray(v) for k, v in data.items()}
    t = {k: nc.dram_tensor("in_" + k, v.shape, F32, kind="ExternalInput").ap() for k, v in data.items()}
    out = nc.dram_tensor("out", (B, LX, E), F32, kind="ExternalOutput").ap()
    build(nc, t["x"], t["ctxT"], {n: t[n] for n in sq}, (t["fc1"], t["fc2"], t["l1w1"], t["l1w2"]), t["cols"],
          t["rows"], t["lnrow"], t["ident"], t["masks"], t["trig"], out)
    r = run_bass_kernel_spmd(nc, [{"in_" + k: v for k, v in data.items()}], core_ids=[0])
    return r.results[0]["out"]
```
